# Optimizing a Trainium2 kernel written in Bass

```python
import numpy as np
import jax
import jax.numpy as jnp

def _softmax(x, axis=-1):
    return jax.nn.softmax(x, axis=axis)

def _gelu(x):
    return jax.nn.gelu(x, approximate=True)

def _silu(x):
    return jax.nn.silu(x)

def _sigmoid(x):
    return jax.nn.sigmoid(x)

def _layernorm(x, axis=-1, eps=1e-05):
    m = jnp.mean(x, axis=axis, keepdims=True)
    v = jnp.var(x, axis=axis, keepdims=True)
    return (x - m) / jnp.sqrt(v + eps)

def _scatter_add(tgt, idx, src, axis=0):
    return tgt.at[idx].add(src)

def _segment_sum(src, seg, n):
    return jax.ops.segment_sum(src, seg, n)
kernel_name = 'mk_vit_tower_postln_d1_tok_img1024_r4_ba3360'

def setup_inputs(seed: int=0):
    np.random.seed(seed)
    _w = jnp.asarray

    def _rec_inputs():
        import jax
        import jax.numpy as jnp
        _rk = jax.random.key(seed)
        x = -0.000222058 + 0.999998 * jax.random.normal(jax.random.fold_in(_rk, 1), (32, 3, 96, 96), jnp.float32)
        return x
    x = _rec_inputs()

    def _L0_tok_setup():
        import jax, jax.numpy as jnp
        import numpy as np
        P = 16
        key = jax.random.key(seed)
        kx, kw, kb = jax.random.split(key, 3)
        B, C, H, W_ = (32, 3, 128, 128)
        in_dim, embed_dim = (C * P * P, 256)
        x = jax.random.normal(kx, (B, C, H, W_), dtype=jnp.float32)
        bound = 1.0 / np.sqrt(in_dim)
        W = jax.random.uniform(kw, (embed_dim, in_dim), minval=-bound, maxval=bound, dtype=jnp.float32)
        b = jax.random.uniform(kb, (embed_dim,), minval=-bound, maxval=bound, dtype=jnp.float32)
        return {'x': x, 'W': W, 'b': b}
    _L0_tok_all = _L0_tok_setup()
    _L0_tok_in = {k: v for k, v in _L0_tok_all.items() if k in ('W', 'b')}
    del _L0_tok_all

    def _L0_attn_setup():
        import jax, jax.numpy as jnp
        import numpy as np
        DIM = 256
        N_HEADS = 16
        HEAD_DIM = DIM // N_HEADS
        SCALE = HEAD_DIM ** (-0.5)
        key = jax.random.key(seed)
        kx, kq, kk, kv = jax.random.split(key, 4)
        x = jax.random.normal(kx, (2, 512, DIM), dtype=jnp.float32)
        bv_q = jax.random.normal(kq, (N_HEADS, HEAD_DIM), dtype=jnp.float32) * 0.02
        bv_k = jax.random.normal(kk, (N_HEADS, HEAD_DIM), dtype=jnp.float32) * 0.02
        bv_v = jax.random.normal(kv, (N_HEADS, HEAD_DIM), dtype=jnp.float32) * 0.02
        return {'x': x, 'bv_q': bv_q, 'bv_k': bv_k, 'bv_v': bv_v}
    _L0_attn_all = _L0_attn_setup()
    _L0_attn_in = {k: v for k, v in _L0_attn_all.items() if k in ('bv_q', 'bv_k', 'bv_v')}
    del _L0_attn_all

    def _L0_ffn_setup():
        import jax, jax.numpy as jnp
        import numpy as np
        from jax import lax
        D = 256
        H = 352
        E = 8
        K = 2
        ROUTER_SCALE = 1.0

        def _expert(x, w1, b1, w3, b3, w2, b2):
            h = jax.nn.silu((x @ w1 + b1) * (x @ w3 + b3))
            return h @ w2 + b2
        key = jax.random.key(seed)
        ks = jax.random.split(key, 16)
        s = 0.02
        inp = {'x': jax.random.normal(ks[0], (2, 512, D), dtype=jnp.float32), 'gate_w': jax.random.normal(ks[1], (E, D), dtype=jnp.float32) * s, 'gate_b': jax.random.normal(ks[2], (E,), dtype=jnp.float32) * s, 'w1': jax.random.normal(ks[3], (E, D, H), dtype=jnp.float32) * s, 'b1': jax.random.normal(ks[4], (E, H), dtype=jnp.float32) * s, 'w3': jax.random.normal(ks[5], (E, D, H), dtype=jnp.float32) * s, 'b3': jax.random.normal(ks[6], (E, H), dtype=jnp.float32) * s, 'w2': jax.random.normal(ks[7], (E, H, D), dtype=jnp.float32) * s, 'b2': jax.random.normal(ks[8], (E, D), dtype=jnp.float32) * s, 'sw1': jax.random.normal(ks[9], (D, H), dtype=jnp.float32) * s, 'sb1': jax.random.normal(ks[10], (H,), dtype=jnp.float32) * s, 'sw3': jax.random.normal(ks[11], (D, H), dtype=jnp.float32) * s, 'sb3': jax.random.normal(ks[12], (H,), dtype=jnp.float32) * s, 'sw2': jax.random.normal(ks[13], (H, D), dtype=jnp.float32) * s, 'sb2': jax.random.normal(ks[14], (D,), dtype=jnp.float32) * s}
        return inp
    _L0_ffn_all = _L0_ffn_setup()
    _L0_ffn_in = {k: v for k, v in _L0_ffn_all.items() if k in ('gate_w', 'gate_b', 'w1', 'b1', 'w3', 'b3', 'w2', 'b2', 'sw1', 'sb1', 'sw3', 'sb3', 'sw2', 'sb2')}
    del _L0_ffn_all
    return {'x': x, 'L0_tok_W': _L0_tok_in['W'], 'L0_tok_b': _L0_tok_in['b'], 'L0_attn_bv_q': _L0_attn_in['bv_q'], 'L0_attn_bv_k': _L0_attn_in['bv_k'], 'L0_attn_bv_v': _L0_attn_in['bv_v'], 'L0_ffn_gate_w': _L0_ffn_in['gate_w'], 'L0_ffn_gate_b': _L0_ffn_in['gate_b'], 'L0_ffn_w1': _L0_ffn_in['w1'], 'L0_ffn_b1': _L0_ffn_in['b1'], 'L0_ffn_w3': _L0_ffn_in['w3'], 'L0_ffn_b3': _L0_ffn_in['b3'], 'L0_ffn_w2': _L0_ffn_in['w2'], 'L0_ffn_b2': _L0_ffn_in['b2'], 'L0_ffn_sw1': _L0_ffn_in['sw1'], 'L0_ffn_sb1': _L0_ffn_in['sb1'], 'L0_ffn_sw3': _L0_ffn_in['sw3'], 'L0_ffn_sb3': _L0_ffn_in['sb3'], 'L0_ffn_sw2': _L0_ffn_in['sw2'], 'L0_ffn_sb2': _L0_ffn_in['sb2']}

def reference(x, L0_tok_W, L0_tok_b, L0_attn_bv_q, L0_attn_bv_k, L0_attn_bv_v, L0_ffn_gate_w, L0_ffn_gate_b, L0_ffn_w1, L0_ffn_b1, L0_ffn_w3, L0_ffn_b3, L0_ffn_w2, L0_ffn_b2, L0_ffn_sw1, L0_ffn_sb1, L0_ffn_sw3, L0_ffn_sb3, L0_ffn_sw2, L0_ffn_sb2):
    import jax
    import jax.numpy as jnp

    def _L0_tok_ref(x, W, b):
        import jax, jax.numpy as jnp
        import numpy as np
        P = 16
        B, C, H, Wd = x.shape
        h, w = (H // P, Wd // P)
        patches = x.reshape(B, C, h, P, w, P).transpose(0, 2, 4, 1, 3, 5)
        patches = patches.reshape(B, h * w, C * P * P)
        return jnp.einsum('bld,ed->ble', patches, W) + b

    def _L0_attn_ref(x, bv_q, bv_k, bv_v):
        import jax, jax.numpy as jnp
        import numpy as np
        DIM = 256
        N_HEADS = 16
        HEAD_DIM = DIM // N_HEADS
        SCALE = HEAD_DIM ** (-0.5)
        B, T, D = x.shape
        H, HD = (N_HEADS, HEAD_DIM)
        x_h = x.reshape(B, T, H, HD)
        Q = x_h * jnp.sign(bv_q)
        K = x_h * jnp.sign(bv_k)
        V = x_h * jnp.sign(bv_v)
        scores = jnp.einsum('bqhd,bkhd->bhqk', Q, K) * SCALE
        causal = jnp.tril(jnp.ones((T, T), dtype=bool))
        attn = jnp.where(causal, jax.nn.sigmoid(scores * 4.0), 0.0)
        out = jnp.einsum('bhqk,bkhd->bqhd', attn, V)
        return out.reshape(B, T, D)

    def _L0_ffn_ref(x, gate_w, gate_b, w1, b1, w3, b3, w2, b2, sw1, sb1, sw3, sb3, sw2, sb2):
        import jax, jax.numpy as jnp
        import numpy as np
        from jax import lax
        D = 256
        H = 352
        E = 8
        K = 2
        ROUTER_SCALE = 1.0

        def _expert(x, w1, b1, w3, b3, w2, b2):
            h = jax.nn.silu((x @ w1 + b1) * (x @ w3 + b3))
            return h @ w2 + b2
        shape = x.shape
        xf = x.reshape(-1, D)
        T = xf.shape[0]
        scores = jax.nn.softmax(xf @ gate_w.T, axis=-1)
        biased = scores + gate_b
        _, idx = lax.top_k(biased, K)
        w = jnp.take_along_axis(scores, idx, axis=-1) * ROUTER_SCALE
        rw = jnp.zeros((T, E), dtype=xf.dtype).at[jnp.arange(T)[:, None], idx].add(w)
        h = jax.nn.silu((jnp.einsum('td,edh->teh', xf, w1) + b1) * (jnp.einsum('td,edh->teh', xf, w3) + b3))
        oe = jnp.einsum('teh,ehd->ted', h, w2) + b2
        y = jnp.einsum('te,ted->td', rw, oe)
        z = _expert(xf, sw1, sb1, sw3, sb3, sw2, sb2)
        return (y + z).reshape(shape)
    h = _L0_tok_ref(x, L0_tok_W, L0_tok_b)
    h = _layernorm(h + _L0_attn_ref(h, L0_attn_bv_q, L0_attn_bv_k, L0_attn_bv_v), axis=-1)
    h = _layernorm(h + _L0_ffn_ref(h, L0_ffn_gate_w, L0_ffn_gate_b, L0_ffn_w1, L0_ffn_b1, L0_ffn_w3, L0_ffn_b3, L0_ffn_w2, L0_ffn_b2, L0_ffn_sw1, L0_ffn_sb1, L0_ffn_sw3, L0_ffn_sb3, L0_ffn_sw2, L0_ffn_sb2), axis=-1)
    return h

_drawn_inputs = setup_inputs


def setup_inputs(seed=0):
    import zlib

    import numpy as np

    out = dict(_drawn_inputs(seed))
    spreads = {}
    factors = {'L0_ffn_gate_w': 8.0,
     'L0_ffn_gate_b': 8.0,
     'L0_ffn_w1': 8.0,
     'L0_ffn_b1': 8.0,
     'L0_ffn_w3': 8.0,
     'L0_ffn_b3': 8.0,
     'L0_ffn_w2': 8.0,
     'L0_ffn_b2': 38.701,
     'L0_ffn_sw1': 2.956,
     'L0_ffn_sb1': 33.375,
     'L0_ffn_sw3': 2.919,
     'L0_ffn_sb3': 35.046,
     'L0_ffn_sw2': 2.947,
     'L0_ffn_sb2': 22.874}
    for name, (base, spread) in spreads.items():
        noise = np.random.default_rng([zlib.crc32(name.encode()), seed]).standard_normal(out[name].shape)
        drawn = base * np.exp(spread * noise) if base else spread * noise
        out[name] = jnp.asarray(drawn.astype(out[name].dtype))
    for name, factor in factors.items():
        out[name] = (out[name] * factor).astype(out[name].dtype)
    return out
```

```python
from contextlib import ExitStack

import concourse.bass as bass
from concourse import mybir

F32 = mybir.dt.float32
BF16 = mybir.dt.bfloat16
I32 = mybir.dt.int32
ALU = mybir.AluOpType
ACT = mybir.ActivationFunctionType
AX = mybir.AxisListType

P = 128
EPS = 1e-5
MASKED = -1e30


def vit_layer(nc, patches_T, tok_wT, tok_b, bq, bk, bv_row, gate_wT, gate_b,
              w1, b1, w3, b3, w2, b2, sw1, sb1, sw3, sb3, sw2, sb2, out):
    K_IN, TOK = patches_T.shape
    D = tok_wT.shape[1]
    IMG = 36
    KC = K_IN // P
    C = D // P
    NH, HD = 16, 16
    HPC = P // HD
    GROUPS = P // 32
    BH = 4
    E, _, HID = w1.shape
    SH = E
    NE = E + 1
    TT = 3 * IMG
    NA = -(-TOK // TT)
    LAST = TOK - (NA - 1) * TT
    CH = 3 * TT
    CHUNKS = [(s, min(CH, TOK - s)) for s in range(0, TOK, CH)]
    NT = TOK // P
    TOP = 2
    R = (TOP * TOK - E) // P + E
    H2 = 2 * HID
    HC = [(s, min(P, HID - s)) for s in range(0, HID, P)]
    NHC = len(HC)

    h1_dram = nc.dram_tensor("h1_rows", (TOK, D), F32).ap()
    y_dram = nc.dram_tensor("y_rows", (R * P, D), F32).ap()

    with ExitStack() as ctx:
        def sb(name, shape, dt=F32):
            return ctx.enter_context(nc.sbuf_tensor(name, shape, dt))

        def sem(name):
            return ctx.enter_context(nc.semaphore(name))

        ident = sb("ident", [P, P])
        ident_bf = sb("ident_bf", [P, P], BF16)
        zeros_tt = sb("zeros_tt", [TT, TT])
        mask_f = sb("mask_f", [TT, TT])
        mask_bf = sb("mask_bf", [TT, TT], BF16)
        before = sb("before", [P, P], BF16)
        ones_bf = sb("ones_bf", [P, P], BF16)
        ones_f = sb("ones_f", [P, P])
        part = sb("part", [P, 1], I32)
        part_f = sb("part_f", [P, 1])
        head_i = sb("head_i", [P, 1], I32)
        head_f = sb("head_f", [P, 1])
        own_head = sb("own_head", [P, HPC])
        iota_row = sb("iota_row", [P, P], I32)
        iota_f = sb("iota_f", [P, P])
        tri_i = sb("tri_i", [P, E, E])
        half_neg = sb("half_neg", [P, 1])
        eps = sb("eps", [P, 1])
        wT = sb("wT", [P, KC, D])
        bias_d = sb("bias_d", [P, C])
        qk = sb("qk", [P, 2, C])
        vrow = sb("vrow", [P, D])
        sgn = sb("sgn", [P, 6, C])
        sgn_qk = sb("sgn_qk", [P, C])
        sel_qk = sb("sel_qk", [P, C, HPC])
        vs = sb("vs", [P, 2, D])
        sgn_v = sb("sgn_v", [P, D])
        gwT = sb("gwT", [P, C, E])
        gb = sb("gb", [P, E])
        w13 = sb("w13", [P, C, NE * H2])
        w2s = sb("w2s", [P, NHC, NE * D])
        hT_acc = sb("hT_acc", [P, C * TOK])
        hT = hT_acc[:, :].rearrange("p (c t) -> p c t", c=C)
        acc = hT_acc[:, :].rearrange("p (t d) -> p t d", t=NT)
        htok = sb("htok", [P, NA, D])
        resid = htok
        h1T = sb("h1T", [P, C, TOK])
        gath = sb("gath", [P, KC * TOK])
        patch = gath[:, :].rearrange("p (k t) -> p k t", k=KC)
        xg = gath[:, 0:2 * D].rearrange("p (u d) -> p u d", u=2)
        yg = gath[:, 0:TOP * NT * D].rearrange("p (t k d) -> p t k d", t=NT, k=TOP)
        fin = gath[:, TOP * NT * D:(TOP * NT + 3) * D].rearrange("p (u d) -> p u d", u=3)
        QN = C * HPC * TT
        AN = NH * TT
        VN = NH * 32
        BIAS_N = NE * (H2 + D)
        scratch = sb("scratch", [P, max(2 * (QN + AN + VN), BIAS_N)])
        qx = [scratch[:, i * QN:(i + 1) * QN].rearrange("p (c h t) -> p c h t", c=C, h=HPC) for i in range(2)]
        att = [scratch[:, 2 * QN + i * AN:2 * QN + (i + 1) * AN].rearrange("p (b x) -> p b x", b=NH // BH)
               for i in range(2)]
        vt = [scratch[:, 2 * (QN + AN) + i * VN:2 * (QN + AN) + (i + 1) * VN] for i in range(2)]
        b13 = scratch[:, 0:NE * H2]
        b2b = scratch[:, NE * H2:BIAS_N]
        zT = sb("zT", [P, 2, C * TT])
        stats = sb("stats", [P, 2, 6])
        mv = sb("mv", [P, 2, 2])
        var_eps = sb("var_eps", [P, 2, 1])
        rstd = sb("rstd", [P, 2, 1])
        route_at = [0]

        def route_f(n):
            route_at[0] += n
            return gath[:, route_at[0] - n:route_at[0]]

        lg = sb("lg", [P, NT, E])
        lmax = sb("lmax", [P, NT])
        lex = sb("lex", [P, NT, E])
        lsum = sb("lsum", [P, NT])
        lrec = sb("lrec", [P, NT])
        probs = sb("probs", [P, NT, E])
        biased = sb("biased", [P, NT, E])
        pair_a = route_f(NT * E * E).rearrange("p (t e j) -> p t e j", t=NT, e=E)
        pair_b = route_f(NT * E * E).rearrange("p (t e j) -> p t e j", t=NT, e=E)
        rank = sb("rank", [P, NT, E])
        hot = sb("hot", [P, TOP, NT, E])
        sel = sb("sel", [P, NT, E], BF16)
        selcum = sb("selcum", [P, NT + 1, E], BF16)
        rw = sb("rw", [P, TOP, NT])
        tmp = sb("tmp", [P, TOP, NT, E])
        full = sb("full", [P, NT])
        cmp_n = sb("cmp_n", [P, E, NT])
        ntile = sb("ntile", [P, E])
        cmp_c = sb("cmp_c", [P, E, E])
        tstart = sb("tstart", [P, E])
        tend = sb("tend", [P, E])
        place = sb("place", [P, NT, E])
        slot_f = sb("slot_f", [P, TOP, NT])
        slot = sb("slot", [P, TOP * NT], I32)
        slot_hi = sb("slot_hi", [P, TOP * NT], I32)
        slot_lo = sb("slot_lo", [P, TOP * NT], I32)
        hi_f = sb("hi_f", [P, TOP * NT])
        lo_f = sb("lo_f", [P, TOP * NT])
        in_tile = route_f(TOP * NT * R).rearrange("p (i r) -> p i r", r=R)
        at_pos = route_f(TOP * NT * P // 2).bitcast(BF16).rearrange("p (i q) -> p i q", q=P)
        ids = route_f(TOP * NT * R).bitcast(BF16).rearrange("p (i r) -> p i r", r=2 * R)
        idx_f = sb("idx_f", [P, 2 * R])
        idx = sb("idx", [P, R], I32)
        cmp_e = route_f(R * E).rearrange("p (r e) -> p r e", e=E)
        eid_f = sb("eid_f", [P, R])
        eid_c = sb("eid_c", [P, R])
        eid = sb("eid", [P, R], I32)
        xT = sb("xT", [P, 2, C * P])
        up1 = sb("up1", [P, HID])
        up3 = sb("up3", [P, HID])
        gated = sb("gated", [P, 2, HID])
        hid = sb("hid", [P, 2, HID])
        hidT = sb("hidT", [P, 2, NHC, P])
        yb = sb("yb", [P, 2, D])

        ps_lo = ctx.enter_context(nc.psum_tensor("ps_lo", [P, 4, 512], F32))
        ps_hi = ctx.enter_context(nc.psum_tensor("ps_hi", [P, 4, 512], F32))

        wT_loaded = sem("wT_loaded")
        small_loaded = sem("small_loaded")
        patch_loaded = [sem(f"patch_loaded{n}") for n in range(len(CHUNKS))]
        weights_loaded = sem("weights_loaded")
        sbias_loaded = sem("sbias_loaded")
        rbias_loaded = sem("rbias_loaded")
        resid_loaded = sem("resid_loaded")
        pool_chain = sem("pool_chain")
        consts_ready = sem("consts_ready")
        dve_chain = sem("dve_chain")
        embed_done = sem("embed_done")
        hT_ready = sem("hT_ready")
        q_ready = sem("q_ready")
        scores_done = sem("scores_done")
        sig_done = sem("sig_done")
        tr_done = sem("tr_done")
        v_ready = sem("v_ready")
        av_done = sem("av_done")
        zT_ready = sem("zT_ready")
        ztr_done = sem("ztr_done")
        stats_ready = sem("stats_ready")
        mv_ready = sem("mv_ready")
        vareps_ready = sem("vareps_ready")
        rstd_ready = sem("rstd_ready")
        h1_ready = sem("h1_ready")
        h1_stored = sem("h1_stored")
        h1tr_done = sem("h1tr_done")
        h1T_ready = sem("h1T_ready")
        logits_done = sem("logits_done")
        shifted_ready = sem("shifted_ready")
        exp_done = sem("exp_done")
        sel_ready = sem("sel_ready")
        prefix_done = sem("prefix_done")
        onehot_ready = sem("onehot_ready")
        index_done = sem("index_done")
        eid_ready = sem("eid_ready")
        idx_ready = sem("idx_ready")
        xg_loaded = [sem(f"xg_loaded{i}") for i in range(2)]
        xtr_done = sem("xtr_done")
        xT_ready = sem("xT_ready")
        mm1_done = sem("mm1_done")
        up1_ready = sem("up1_ready")
        up3_ready = sem("up3_ready")
        gated_ready = sem("gated_ready")
        hid_ready = sem("hid_ready")
        htr_done = sem("htr_done")
        hidT_ready = sem("hidT_ready")
        mm2_done = sem("mm2_done")
        y_ready = sem("y_ready")
        acc_ready = sem("acc_ready")
        y_stored = [sem(f"y_stored{i}") for i in range(2)]
        yg_loaded = [sem(f"yg_loaded{i}") for i in range(3)]
        mix0_ready = sem("mix0_ready")
        mix_ready = sem("mix_ready")
        stats2_ready = sem("stats2_ready")
        mv2_ready = sem("mv2_ready")
        vareps2_ready = sem("vareps2_ready")
        rstd2_ready = sem("rstd2_ready")
        final_ready = sem("final_ready")
        out_stored = [sem(f"out_stored{i}") for i in range(3)]

        SF = 4
        RL = SF + R
        NS = NT + R
        LOOP0, LOOP1 = SF + 4, SF + 4 + (RL - 1 - SF - 4) // 2 * 2

        def routed(n):
            return not isinstance(n, int) or SF <= n < RL

        def shared_tile(n):
            return n if n < SF else n - R

        def small_inputs():
            return [(bias_d[:, :], tok_b), (qk[:, 0, :], bq), (qk[:, 1, :], bk),
                    (vrow[:, :], bv_row.partition_broadcast(P)),
                    (gwT[:, :, :], gate_wT.rearrange("(c p) e -> p c e", p=P)),
                    (gb[:, :], gate_b.partition_broadcast(P))]

        block = ctx.enter_context(nc.Block())

        @block.sync
        def _(sp):
            sp.dma_start(wT[:, :, :], tok_wT.rearrange("(k p) d -> p k d", p=P)).then_inc(wT_loaded, 16)
            for n, (s, m) in enumerate(CHUNKS):
                sp.dma_start(patch[:, :, s:s + m],
                             patches_T[:, s:s + m].rearrange("(k p) t -> p k t", p=P)).then_inc(patch_loaded[n], 16)
                if n == 0:
                    for dst, src in small_inputs():
                        sp.dma_start(dst, src).then_inc(small_loaded, 16)
            for e, (a, c, d) in [(SH, (sw1, sw3, sw2))] + [(e, (w1[e], w3[e], w2[e])) for e in range(E)]:
                for i, w in enumerate((a, c)):
                    sp.dma_start(w13[:, :, e * H2 + i * HID:e * H2 + (i + 1) * HID],
                                 w.rearrange("(c p) n -> p c n", p=P)).then_inc(weights_loaded, 16)
                full_rows = (HID // P) * P
                sp.dma_start(w2s[:, 0:HID // P, e * D:(e + 1) * D],
                             d[0:full_rows, :].rearrange("(c p) n -> p c n", p=P)).then_inc(weights_loaded, 16)
                sp.dma_start(w2s[0:HID - full_rows, NHC - 1, e * D:(e + 1) * D],
                             d[full_rows:HID, :]).then_inc(weights_loaded, 16)
            with sp.Fori(0, NA - 1) as t:
                sp.wait_ge(h1_ready, t + 1)
                sp.dma_start(h1_dram[bass.ds(t * TT, TT), :], htok[0:TT, bass.ds(t, 1), :]).then_inc(h1_stored, 16)
            sp.wait_ge(h1_ready, NA)
            sp.dma_start(h1_dram[(NA - 1) * TT:TOK, :], htok[0:LAST, NA - 1, :]).then_inc(h1_stored, 16)
            sp.wait_ge(av_done, NA)
            for i, b in enumerate((sb1, sb3)):
                sp.dma_start(b13[:, SH * H2 + i * HID:SH * H2 + (i + 1) * HID],
                             b.partition_broadcast(P)).then_inc(sbias_loaded, 16)
            sp.dma_start(b2b[:, SH * D:(SH + 1) * D], sb2.partition_broadcast(P)).then_inc(sbias_loaded, 16)
            for i, b in enumerate((b1, b3)):
                sp.dma_start(b13[:, 0:E * H2].rearrange("p (e x) -> p e x", e=E)[:, :, i * HID:(i + 1) * HID],
                             b.partition_broadcast(P)).then_inc(rbias_loaded, 16)
            sp.dma_start(b2b[:, 0:E * D].rearrange("p (e x) -> p e x", e=E),
                         b2.partition_broadcast(P)).then_inc(rbias_loaded, 16)
            sp.wait_ge(h1_stored, 16 * NA)
            sp.wait_ge(h1tr_done, NA)
            sp.dma_start(resid[:, 0:NT, :], h1_dram.rearrange("(t p) d -> p t d", p=P)).then_inc(resid_loaded, 16)

            def store_y(r, u):
                sp.wait_ge(y_ready, r + SF + 1)
                sp.dma_start(y_dram[bass.ds(r * P, P), :], yb[:, u, :]).then_inc(y_stored[u], 16)

            with sp.Fori(0, R - 2, 2) as r:
                store_y(r, 0)
                store_y(r + 1, 1)
            store_y(R - 1, 0)
            with sp.Fori(0, NT - 2, 3) as t:
                for u in range(3):
                    sp.wait_ge(final_ready, t + u + 1)
                    sp.dma_start(out[bass.ds((t + u) * P, P), :], fin[:, u, :]).then_inc(out_stored[u], 16)
            for u in range(3):
                sp.wait_ge(out_stored[u], 16 * (NT // 3))

        @block.gpsimd
        def _(pool):
            chain = [0]

            def link(ins):
                chain[0] += 1
                ins.then_inc(pool_chain, 1)
                pool.wait_ge(pool_chain, chain[0])

            nc.gpsimd.memset(half_neg[:, :], -0.5)
            nc.gpsimd.memset(eps[:, :], EPS)
            nc.gpsimd.iota(part[:, :], [[0, 1]], base=0, channel_multiplier=1)
            nc.gpsimd.iota(iota_row[:, :], [[1, P]], base=0, channel_multiplier=0)
            nc.gpsimd.memset(zeros_tt[:, :], 0.0)
            link(nc.gpsimd.memset(ones_f[:, :], 1.0))
            nc.gpsimd.affine_select(out=ident[:, :], in_=ones_f[:, :], compare_op=ALU.is_equal, fill=0.0, base=0,
                                    pattern=[[-1, P]], channel_multiplier=1)
            nc.gpsimd.affine_select(out=before[:, :], in_=ones_f[:, :], compare_op=ALU.is_gt, fill=0.0, base=0,
                                    pattern=[[1, P]], channel_multiplier=-1)
            nc.gpsimd.affine_select(out=tri_i[:, :, :], in_=ones_f[:, 0:E * E].rearrange("p (e j) -> p e j", e=E),
                                    compare_op=ALU.is_gt, fill=0.0, base=0,
                                    pattern=[[1, E], [-1, E]], channel_multiplier=0)
            link(nc.gpsimd.affine_select(out=mask_f[:, :], in_=zeros_tt[:, :], compare_op=ALU.is_ge, fill=MASKED,
                                         base=0, pattern=[[1, TT]], channel_multiplier=-1))
            link(nc.gpsimd.affine_select(out=mask_bf[:, :].rearrange("p (a q) -> p a q", q=IMG),
                                         in_=mask_f[:, :].rearrange("p (a q) -> p a q", q=IMG),
                                         compare_op=ALU.is_ge, fill=MASKED, base=0,
                                         pattern=[[-IMG, TT // IMG], [0, IMG]], channel_multiplier=1))
            nc.gpsimd.tensor_copy(ident_bf[:, :], ident[:, :])
            nc.gpsimd.tensor_copy(ones_bf[:, :], ones_f[:, :])
            nc.gpsimd.tensor_copy(iota_f[:, :], iota_row[:, :])
            link(nc.gpsimd.tensor_copy(part_f[:, :], part[:, :]))
            nc.gpsimd.memset(selcum[:, 0, :], 0.0).then_inc(consts_ready, 1)

            def inverse_deviation(t, u, rows, mvs, vareps, done):
                pool.wait_ge(mvs, t + 1)
                nc.gpsimd.tensor_tensor(var_eps[0:rows, u, :], mv[0:rows, u, 1:2], eps[0:rows, :],
                                        ALU.add).then_inc(vareps, 1)
                pool.wait_ge(vareps, t + 1)
                nc.gpsimd.tensor_tensor(rstd[0:rows, u, :], var_eps[0:rows, u, :], half_neg[0:rows, :],
                                        ALU.pow).then_inc(done, 1)

            with pool.Fori(0, NA - 2, 2) as t:
                inverse_deviation(t, 0, TT, mv_ready, vareps_ready, rstd_ready)
                inverse_deviation(t + 1, 1, TT, mv_ready, vareps_ready, rstd_ready)
            inverse_deviation(NA - 1, 0, LAST, mv_ready, vareps_ready, rstd_ready)

            pool.wait_ge(idx_ready, 1)
            pool.wait_ge(h1_stored, 16 * NA)
            for r in range(R):
                if r >= 2:
                    pool.wait_ge(xg_loaded[r % 2], 16 * (r // 2))
                    pool.wait_ge(xtr_done, r - 1)
                nc.gpsimd.indirect_dma_start(
                    out=xg[:, r % 2, :], out_offset=None, in_=h1_dram,
                    in_offset=bass.IndirectOffsetOnAxis(ap=idx[:, r:r + 1], axis=0),
                ).then_inc(xg_loaded[r % 2], 16)
            pool.wait_ge(y_stored[0], 16 * ((R + 1) // 2))
            pool.wait_ge(y_stored[1], 16 * (R // 2))

            def final_tile(t):
                inverse_deviation(t, t % 2, P, mv2_ready, vareps2_ready, rstd2_ready)

            for t in range(NT):
                if t >= 3:
                    pool.wait_ge(yg_loaded[t % 3], 16 * TOP * (t // 3))
                for k in range(TOP):
                    nc.gpsimd.indirect_dma_start(
                        out=yg[:, t, k, :], out_offset=None, in_=y_dram,
                        in_offset=bass.IndirectOffsetOnAxis(ap=slot[:, k * NT + t:k * NT + t + 1], axis=0),
                    ).then_inc(yg_loaded[t % 3], 16)
                if t >= 3:
                    final_tile(t - 3)
            for t in range(NT - 3, NT):
                final_tile(t)

        @block.scalar
        def _(act):
            act.wait_ge(small_loaded, 16 * len(small_inputs()))
            for n, (s, m) in enumerate(CHUNKS):
                for c in range(C):
                    act.wait_ge(embed_done, C * n + c + 1)
                    nc.scalar.activation(hT[:, c, s:s + m], ps_hi[:, (n % 2) * C + c, 0:m], ACT.Identity,
                                         bias=bias_d[:, c:c + 1]).then_inc(hT_ready, 1)

            def sigmoid(t, u, rows):
                act.wait_ge(scores_done, t + 1)
                if not isinstance(t, int) or t >= 2:
                    act.wait_ge(av_done, t - 1)
                nc.scalar.activation(
                    att[u][0:rows, :, 0:BH * rows], ps_lo[0:rows, :, 0:BH * rows],
                    ACT.Sigmoid).then_inc(sig_done, 1)

            def keep_h1T(t, rows):
                act.wait_ge(h1tr_done, t + 1)
                nc.scalar.activation(h1T[:, :, bass.ds(t * TT, rows)],
                                     ps_hi[:, 3, 0:C * rows].rearrange("p (c t) -> p c t", c=C),
                                     ACT.Copy).then_inc(h1T_ready, 1)

            sigmoid(0, 0, TT)
            sigmoid(1, 1, TT)
            sigmoid(2, 0, TT)
            with act.Fori(2, NA - 4, 2) as t:
                sigmoid(t + 1, 1, TT)
                keep_h1T(t - 2, TT)
                sigmoid(t + 2, 0, TT)
                keep_h1T(t - 1, TT)
            sigmoid(NA - 2, 1, TT)
            keep_h1T(NA - 5, TT)
            sigmoid(NA - 1, 0, LAST)
            keep_h1T(NA - 4, TT)
            keep_h1T(NA - 3, TT)
            keep_h1T(NA - 2, TT)
            keep_h1T(NA - 1, LAST)

            act.wait_ge(shifted_ready, 1)
            nc.scalar.activation(lex[:, :, :], lg[:, :, :], ACT.Exp).then_inc(exp_done, 1)

            def keep_xT(n, u):
                r = n - SF
                act.wait_ge(xtr_done, r + 1)
                act.wait_ge(mm1_done, n - 1)
                nc.scalar.activation(xT[:, u, :], ps_hi[:, 0, 0:C * P], ACT.Copy).then_inc(xT_ready, 1)

            def silu(n, u):
                act.wait_ge(gated_ready, n + 1)
                if not isinstance(n, int) or n >= 2:
                    act.wait_ge(htr_done, n - 1)
                nc.scalar.activation(hid[:, u, :], gated[:, u, :], ACT.Silu).then_inc(hid_ready, 1)

            def keep_hidT(n, u):
                act.wait_ge(htr_done, n + 1)
                if not isinstance(n, int) or n >= 2:
                    act.wait_ge(mm2_done, n - 1)
                nc.scalar.activation(hidT[:, u, 0:NHC - 1, :], ps_hi[:, 1, 0:(NHC - 1) * P], ACT.Copy)
                rows = HC[-1][1]
                nc.scalar.activation(hidT[0:rows, u, NHC - 1, :], ps_hi[0:rows, 1, (NHC - 1) * P:NHC * P],
                                     ACT.Copy).then_inc(hidT_ready, 1)

            def step(n, u):
                if not isinstance(n, int) or SF <= n + 1 < RL:
                    keep_xT(n + 1, 1 - u)
                if not isinstance(n, int) or 1 <= n <= NS:
                    keep_hidT(n - 1, 1 - u)
                if not isinstance(n, int) or n < NS:
                    silu(n, u)

            for n in range(LOOP0):
                step(n, n % 2)
            with act.Fori(LOOP0, LOOP1 - 1, 2) as n:
                step(n, 0)
                step(n + 1, 1)
            for n in range(LOOP1, NS + 1):
                step(n, n % 2)

        @block.vector
        def _(dve):
            chain = [0]

            def link(ins):
                chain[0] += 1
                ins.then_inc(dve_chain, 1)
                dve.wait_ge(dve_chain, chain[0])

            v = nc.vector
            dve.wait_ge(consts_ready, 1)
            link(v.tensor_scalar(head_i[:, :], part[:, :], 4, None, ALU.arith_shift_right))
            link(v.tensor_copy(head_f[:, :], head_i[:, :]))
            v.tensor_scalar(own_head[:, :], iota_f[:, 0:HPC], head_f[:, :], None, ALU.is_equal)
            v.tensor_scalar(full[:, :], iota_f[:, 0:NT], float(P), None, ALU.mult)
            dve.wait_ge(small_loaded, 16 * len(small_inputs()))
            for i in range(2):
                v.tensor_scalar(sgn[:, i, :], qk[:, i, :], 0.0, None, ALU.is_gt)
                v.tensor_scalar(sgn[:, 2 + i, :], qk[:, i, :], 0.0, None, ALU.is_lt)
            v.tensor_scalar(vs[:, 0, :], vrow[:, :], 0.0, None, ALU.is_gt)
            link(v.tensor_scalar(vs[:, 1, :], vrow[:, :], 0.0, None, ALU.is_lt))
            link(v.tensor_tensor(sgn[:, 4:6, :], sgn[:, 0:2, :], sgn[:, 2:4, :], ALU.subtract))
            link(v.tensor_tensor(sgn_v[:, :], vs[:, 0, :], vs[:, 1, :], ALU.subtract))
            link(v.tensor_tensor(sgn_qk[:, :], sgn[:, 4, :], sgn[:, 5, :], ALU.mult))
            for c in range(C):
                last = v.tensor_scalar(sel_qk[:, c, :], own_head[:, :], sgn_qk[:, c:c + 1], None, ALU.mult)
            link(last)

            def queries(t, u, rows):
                if not isinstance(t, int) or t >= 2:
                    dve.wait_ge(scores_done, t - 1)
                for c in range(C):
                    last = v.tensor_tensor(qx[u][:, c, :, 0:rows],
                                           hT[:, bass.ds(c, 1), bass.ds(t * TT, rows)].broadcast_to([P, HPC, rows]),
                                           sel_qk[:, c, :].unsqueeze(2).broadcast_to([P, HPC, rows]), ALU.mult)
                last.then_inc(q_ready, 1)

            def values(t, u, rows):
                dve.wait_ge(tr_done, t + 1)
                if not isinstance(t, int) or t >= 2:
                    dve.wait_ge(av_done, t - 1)
                heads = vt[u][0:rows, :].rearrange("p (h x) -> p h x", x=64)
                for j in range(2):
                    last = v.tensor_tensor(heads[:, :, 48 * j:48 * j + HD],
                                           ps_hi[0:rows, 2, 0:D].rearrange("p (h j x) -> p h j x", j=2, x=HD)[:, :, j, :],
                                           sgn_v[0:rows, :].rearrange("p (h j x) -> p h j x", j=2, x=HD)[:, :, j, :],
                                           ALU.mult)
                last.then_inc(v_ready, 1)

            def residual(t, u, rows):
                dve.wait_ge(av_done, t + 1)
                if not isinstance(t, int) or t >= 2:
                    dve.wait_ge(ztr_done, t - 1)
                v.tensor_tensor(zT[:, u, 0:C * rows].rearrange("p (c t) -> p c t", c=C),
                                ps_hi[:, 0, 0:C * rows].rearrange("p (c t) -> p c t", c=C),
                                hT[:, :, bass.ds(t * TT, rows)], ALU.add).then_inc(zT_ready, 1)

            def moments(t, u, rows):
                dve.wait_ge(ztr_done, t + 1)
                v.bn_stats(stats[0:rows, u, :], ps_hi[0:rows, 1, 0:D]).then_inc(stats_ready, 1)
                dve.wait_ge(consts_ready, 1)
                dve.wait_ge(stats_ready, t + 1)
                v.bn_aggr(mv[0:rows, u, :], stats[0:rows, u, :]).then_inc(mv_ready, 1)

            def normalise(t, u, rows):
                dve.wait_ge(rstd_ready, t + 1)
                v.tensor_scalar(htok[0:rows, bass.ds(t, 1), :], ps_hi[0:rows, 1, 0:D],
                                mv[0:rows, u, 0:1], rstd[0:rows, u, :], ALU.subtract,
                                ALU.mult).then_inc(h1_ready, 1)

            def tile(t, u, rows, next_rows, after_rows=TT):
                if after_rows:
                    queries(t + 2, u, after_rows)
                if next_rows:
                    values(t + 1, 1 - u, next_rows)
                if not isinstance(t, int) or t >= 1:
                    moments(t - 1, 1 - u, TT)
                residual(t, u, rows)
                if not isinstance(t, int) or t >= 1:
                    normalise(t - 1, 1 - u, TT)

            for i in range(2):
                link(v.memset(vt[i][:, :], 0.0))
            dve.wait_ge(hT_ready, C * len(CHUNKS))
            queries(0, 0, TT)
            queries(1, 1, TT)
            values(0, 0, TT)
            tile(0, 0, TT, TT)
            with dve.Fori(1, NA - 5, 2) as t:
                tile(t, 1, TT, TT)
                tile(t + 1, 0, TT, TT)
            tile(NA - 4, 1, TT, TT)
            tile(NA - 3, 0, TT, TT, LAST)
            tile(NA - 2, 1, TT, LAST, 0)
            tile(NA - 1, 0, LAST, 0, 0)
            moments(NA - 1, 0, LAST)
            normalise(NA - 1, 0, LAST)

            dve.wait_ge(logits_done, 1)
            link(v.tensor_copy(lg[:, :, :], ps_hi[:, 2, 0:NT * E]))
            link(v.tensor_reduce(lmax[:, :], lg[:, :, :], AX.X, ALU.max))
            v.tensor_tensor(lg[:, :, :], lg[:, :, :], lmax[:, :].unsqueeze(2).broadcast_to([P, NT, E]),
                            ALU.subtract).then_inc(shifted_ready, 1)
            dve.wait_ge(exp_done, 1)
            link(v.tensor_reduce(lsum[:, :], lex[:, :, :], AX.X, ALU.add))
            link(v.reciprocal(lrec[:, :], lsum[:, :]))
            link(v.tensor_tensor(probs[:, :, :], lex[:, :, :], lrec[:, :].unsqueeze(2).broadcast_to([P, NT, E]),
                                 ALU.mult))
            link(v.tensor_tensor(biased[:, :, :], probs[:, :, :], gb[:, :].unsqueeze(1).broadcast_to([P, NT, E]),
                                 ALU.add))
            other = biased[:, :, :].unsqueeze(2).broadcast_to([P, NT, E, E])
            own = biased[:, :, :].unsqueeze(3).broadcast_to([P, NT, E, E])
            v.tensor_tensor(pair_a[:, :, :, :], other, own, ALU.is_gt)
            link(v.tensor_tensor(pair_b[:, :, :, :], other, own, ALU.is_equal))
            link(v.tensor_tensor(pair_b[:, :, :, :], pair_b[:, :, :, :],
                                 tri_i[:, :, :].unsqueeze(1).broadcast_to([P, NT, E, E]), ALU.mult))
            link(v.tensor_tensor(pair_a[:, :, :, :], pair_a[:, :, :, :], pair_b[:, :, :, :], ALU.add))
            link(v.tensor_reduce(rank[:, :, :], pair_a[:, :, :, :], AX.X, ALU.add))
            for k in range(TOP):
                v.tensor_scalar(hot[:, k, :, :], rank[:, :, :], float(k), None, ALU.is_equal)
            link(v.tensor_scalar(sel[:, :, :], rank[:, :, :], float(TOP), None, ALU.is_lt))
            for t in range(NT):
                link(v.tensor_tensor(selcum[:, t + 1, :], selcum[:, t, :], sel[:, t, :], ALU.add))
            v.tensor_tensor(tmp[:, :, :, :], hot[:, :, :, :],
                            probs[:, :, :].unsqueeze(1).broadcast_to([P, TOP, NT, E]),
                            ALU.mult).then_inc(sel_ready, 1)
            dve.wait_ge(sel_ready, 1)
            link(v.tensor_reduce(rw[:, :, :], tmp[:, :, :, :], AX.X, ALU.add))

            def gate(n, u):
                if routed(n):
                    e = dve.value_load(eid[0:1, bass.ds(n - SF, 1)], min_val=0, max_val=E - 1)
                else:
                    e = SH
                dve.wait_ge(mm1_done, n + 1)
                if not isinstance(n, int) or n >= 1:
                    dve.wait_ge(gated_ready, n)
                v.tensor_tensor(up1[:, :], ps_lo[:, u * 2, 0:HID], b13[:, bass.ds(e * H2, HID)],
                                ALU.add).then_inc(up1_ready, 1)
                v.tensor_tensor(up3[:, :], ps_lo[:, u * 2 + 1, 0:HID], b13[:, bass.ds(e * H2 + HID, HID)],
                                ALU.add).then_inc(up3_ready, 1)
                dve.wait_ge(up1_ready, n + 1)
                dve.wait_ge(up3_ready, n + 1)
                if not isinstance(n, int) or n >= 2:
                    dve.wait_ge(hid_ready, n - 1)
                v.tensor_tensor(gated[:, u, :], up1[:, :], up3[:, :], ALU.mult).then_inc(gated_ready, 1)

            def keep_y(n, u):
                dve.wait_ge(mm2_done, n + 1)
                if routed(n):
                    r = n - SF
                    e = dve.value_load(eid[0:1, bass.ds(r, 1)], min_val=0, max_val=E - 1)
                    if not isinstance(n, int) or r >= 2:
                        dve.wait_ge(y_stored[u], r // 2 * 16 if isinstance(n, int) else (r - u) * 8)
                    v.tensor_tensor(yb[:, u, :], ps_hi[:, 3, 0:D], b2b[:, bass.ds(e * D, D)],
                                    ALU.add).then_inc(y_ready, 1)
                else:
                    t = shared_tile(n)
                    v.tensor_tensor(acc[:, t, :], ps_hi[:, 3, 0:D], b2b[:, SH * D:(SH + 1) * D],
                                    ALU.add).then_inc(y_ready, 1)
                    dve.wait_ge(y_ready, n + 1)
                    if n == 0:
                        dve.wait_ge(resid_loaded, 16)
                    v.tensor_tensor(acc[:, t, :], acc[:, t, :], resid[:, t, :], ALU.add).then_inc(acc_ready, 1)

            def step(n, u):
                if not isinstance(n, int) or n < NS:
                    gate(n, u)
                if not isinstance(n, int) or n >= 2:
                    keep_y(n - 2, u)

            def find_slots():
                dve.wait_ge(prefix_done, 1)
                count = ps_hi[:, 2, NT * E:NT * E + E]
                link(v.tensor_tensor(cmp_n[:, :, :], count.unsqueeze(2).broadcast_to([P, E, NT]),
                                     full[:, :].unsqueeze(1).broadcast_to([P, E, NT]), ALU.is_gt))
                link(v.tensor_reduce(ntile[:, :], cmp_n[:, :, :], AX.X, ALU.add))
                link(v.tensor_tensor(cmp_c[:, :, :], ntile[:, :].unsqueeze(1).broadcast_to([P, E, E]),
                                     tri_i[:, :, :], ALU.mult))
                link(v.tensor_reduce(tstart[:, :], cmp_c[:, :, :], AX.X, ALU.add))
                link(v.tensor_tensor(tend[:, :], tstart[:, :], ntile[:, :], ALU.add))
                link(v.tensor_tensor(cmp_e[:, :, :], iota_f[:, 0:R].unsqueeze(2).broadcast_to([P, R, E]),
                                     tend[:, :].unsqueeze(1).broadcast_to([P, R, E]), ALU.is_ge))
                link(v.tensor_reduce(eid_f[:, :], cmp_e[:, :, :], AX.X, ALU.add))
                link(v.tensor_scalar(eid_c[:, :], eid_f[:, :], float(E - 1), None, ALU.min))
                v.tensor_copy(eid[:, :], eid_c[:, :]).then_inc(eid_ready, 1)
                link(v.tensor_scalar(tstart[:, :], tstart[:, :], float(P), None, ALU.mult))
                link(v.tensor_tensor(place[:, :, :], ps_hi[:, 2, 0:NT * E].rearrange("p (t e) -> p t e", e=E),
                                     tstart[:, :].unsqueeze(1).broadcast_to([P, NT, E]), ALU.add))
                link(v.tensor_tensor(tmp[:, :, :, :], hot[:, :, :, :],
                                     place[:, :, :].unsqueeze(1).broadcast_to([P, TOP, NT, E]), ALU.mult))
                link(v.tensor_reduce(slot_f[:, :, :], tmp[:, :, :, :], AX.X, ALU.add))
                link(v.tensor_copy(slot[:, :], slot_f[:, :, :].rearrange("p k t -> p (k t)")))
                v.tensor_scalar(slot_hi[:, :], slot[:, :], 7, None, ALU.arith_shift_right)
                link(v.tensor_scalar(slot_lo[:, :], slot[:, :], P - 1, None, ALU.bitwise_and))
                v.tensor_copy(hi_f[:, :], slot_hi[:, :])
                link(v.tensor_copy(lo_f[:, :], slot_lo[:, :]))
                n = TOP * NT
                v.tensor_tensor(at_pos[:, :, :], iota_f[:, :].unsqueeze(1).broadcast_to([P, n, P]),
                                lo_f[:, :].unsqueeze(2).broadcast_to([P, n, P]), ALU.is_equal)
                link(v.tensor_tensor(in_tile[:, :, :], iota_f[:, 0:R].unsqueeze(1).broadcast_to([P, n, R]),
                                     hi_f[:, :].unsqueeze(2).broadcast_to([P, n, R]), ALU.is_equal))
                v.tensor_scalar(ids[:, :, 0:R], in_tile[:, :, :], part_f[:, :], None, ALU.mult)
                for k in range(TOP):
                    last = v.tensor_tensor(ids[:, k * NT:(k + 1) * NT, R:2 * R], in_tile[:, k * NT:(k + 1) * NT, :],
                                           iota_f[:, 0:NT].unsqueeze(2).broadcast_to([P, NT, R]), ALU.mult)
                last.then_inc(onehot_ready, 1)

            def find_tokens():
                dve.wait_ge(index_done, 1)
                link(v.tensor_copy(idx_f[:, :], ps_hi[:, 2, 0:2 * R]))
                link(v.scalar_tensor_tensor(out=idx_f[:, 0:R], in0=idx_f[:, R:2 * R], scalar=float(P),
                                            in1=idx_f[:, 0:R], op0=ALU.mult, op1=ALU.add))
                v.tensor_copy(idx[:, :], idx_f[:, 0:R]).then_inc(idx_ready, 1)

            dve.wait_ge(sbias_loaded, 16 * 3)
            for n in range(LOOP0):
                if n == SF:
                    dve.wait_ge(eid_ready, 1)
                    dve.wait_ge(rbias_loaded, 16 * 3)
                step(n, n % 2)
                if n == 0:
                    find_slots()
                if n == 1:
                    find_tokens()
            with dve.Fori(LOOP0, LOOP1 - 1, 2) as n:
                step(n, 0)
                step(n + 1, 1)
            for n in range(LOOP1, NS + 2):
                step(n, n % 2)

            def combine(t, u, first):
                dve.wait_ge(yg_loaded[u], (t - u) // 3 * 32 + 32 if isinstance(t, int) else (t - u + 3) * 32 // 3)
                v.scalar_tensor_tensor(out=acc[:, t, :], in0=yg[:, t, 0, :], scalar=rw[:, 0, t:t + 1],
                                       in1=acc[:, t, :], op0=ALU.mult, op1=ALU.add).then_inc(mix0_ready, 1)
                dve.wait_ge(mix0_ready, t + 1)
                v.scalar_tensor_tensor(out=acc[:, t, :], in0=yg[:, t, 1, :], scalar=rw[:, 1, t:t + 1],
                                       in1=acc[:, t, :], op0=ALU.mult, op1=ALU.add).then_inc(mix_ready, 1)
                dve.wait_ge(mix_ready, t + 1)
                v.bn_stats(stats[:, t % 2, :], acc[:, t, :]).then_inc(stats2_ready, 1)
                dve.wait_ge(stats2_ready, t + 1)
                v.bn_aggr(mv[:, t % 2, :], stats[:, t % 2, :]).then_inc(mv2_ready, 1)

            def finish(t):
                dve.wait_ge(rstd2_ready, t + 1)
                if t >= 3:
                    dve.wait_ge(out_stored[t % 3], 16 * (t // 3))
                v.tensor_scalar(fin[:, t % 3, :], acc[:, t, :], mv[:, t % 2, 0:1], rstd[:, t % 2, :],
                                ALU.subtract, ALU.mult).then_inc(final_ready, 1)

            dve.wait_ge(acc_ready, NT)
            for t in range(NT):
                combine(t, t % 3, t)
                if t >= 1:
                    finish(t - 1)
            finish(NT - 1)

        @block.tensor
        def _(pe):
            mm = nc.tensor.matmul
            pe.wait_ge(wT_loaded, 16)
            for n, (s, m) in enumerate(CHUNKS):
                pe.wait_ge(patch_loaded[n], 16)
                if n >= 2:
                    pe.wait_ge(hT_ready, C * (n - 1))
                for c in range(C):
                    for k in range(KC):
                        last = mm(ps_hi[:, (n % 2) * C + c, 0:m], wT[:, k, c * P:(c + 1) * P], patch[:, k, s:s + m],
                                  start=(k == 0), stop=(k == KC - 1))
                    last.then_inc(embed_done, 1)

            def scores(t, rows):
                if not isinstance(t, int) or t >= 1:
                    pe.wait_ge(sig_done, t)
                pe.wait_ge(q_ready, t + 1)
                for b in range(NH // BH):
                    c, h = b * BH // HPC, b * BH % HPC
                    bank = ps_lo[0:rows, b, 0:BH * rows].rearrange("p (h q) -> p h q", h=BH)
                    mm(bank, ident_bf[0:rows, 0:rows],
                       mask_bf[0:rows, 0:rows].unsqueeze(1).broadcast_to([rows, BH, rows]), start=True, stop=False)
                    last = mm(bank, hT[:, c, t * TT:t * TT + rows], qx[t % 2][:, c, h:h + BH, 0:rows],
                              start=False, stop=True)
                last.then_inc(scores_done, 1)

            def to_tokens(t, rows):
                if t >= 1:
                    pe.wait_ge(v_ready, t)
                for c in range(C):
                    last = nc.tensor.transpose(ps_hi[0:rows, 2, c * P:(c + 1) * P], hT[:, c, bass.ds(t * TT, rows)],
                                               ident[:, :])
                last.then_inc(tr_done, 1)

            def attend(t, u, rows):
                pe.wait_ge(sig_done, t + 1)
                pe.wait_ge(v_ready, t + 1)
                if t >= 1:
                    pe.wait_ge(zT_ready, t)
                for c in range(C):
                    for j in range(2):
                        for g in range(GROUPS):
                            h = (c * GROUPS + g) * 2 + j
                            x = h % BH * rows
                            last = mm(ps_hi[32 * g:32 * g + 32, 0, c * rows:(c + 1) * rows],
                                      vt[u][0:rows, h * 32:(h + 1) * 32], att[u][0:rows, h // BH, x:x + rows],
                                      start=(j == 0), stop=(j == 1))
                last.then_inc(av_done, 1)

            def z_transpose(t, u, rows):
                pe.wait_ge(zT_ready, t + 1)
                if t >= 1:
                    pe.wait_ge(h1_ready, t)
                for c in range(C):
                    last = nc.tensor.transpose(ps_hi[0:rows, 1, c * P:(c + 1) * P],
                                               zT[:, u, c * rows:(c + 1) * rows], ident[:, :])
                last.then_inc(ztr_done, 1)

            def h1_transpose(t, rows):
                pe.wait_ge(h1_ready, t + 1)
                if not isinstance(t, int) or t >= 1:
                    pe.wait_ge(h1T_ready, t)
                for c in range(C):
                    last = nc.tensor.transpose(ps_hi[:, 3, c * rows:(c + 1) * rows],
                                               htok[0:rows, bass.ds(t, 1), c * P:(c + 1) * P], ident[0:rows, 0:rows])
                last.then_inc(h1tr_done, 1)

            pe.wait_ge(consts_ready, 1)
            pe.wait_ge(hT_ready, C * len(CHUNKS))
            rows = [TT] * (NA - 1) + [LAST]
            scores(0, TT)
            to_tokens(0, TT)
            for t in range(NA):
                if t + 1 < NA:
                    to_tokens(t + 1, rows[t + 1])
                    scores(t + 1, rows[t + 1])
                if t >= 1:
                    z_transpose(t - 1, (t - 1) % 2, TT)
                attend(t, t % 2, rows[t])
                if t >= 2:
                    h1_transpose(t - 2, TT)
            z_transpose(NA - 1, (NA - 1) % 2, LAST)
            h1_transpose(NA - 2, TT)
            h1_transpose(NA - 1, LAST)

            pe.wait_ge(h1T_ready, NA)
            for t in range(NT):
                for c in range(C):
                    last = mm(ps_hi[:, 2, t * E:(t + 1) * E], h1T[:, c, t * P:(t + 1) * P], gwT[:, c, :],
                              start=(c == 0), stop=(c == C - 1))
            last.then_inc(logits_done, 1)

            def x_transpose(n, u):
                r = n - SF
                pe.wait_ge(xg_loaded[u], 16 * (r // 2 + 1) if isinstance(n, int) else (r - u + 2) * 8)
                if not isinstance(n, int) or r >= 1:
                    pe.wait_ge(xT_ready, r)
                for c in range(C):
                    last = nc.tensor.transpose(ps_hi[:, 0, c * P:(c + 1) * P],
                                               xg[:, u, c * P:(c + 1) * P], ident[:, :])
                last.then_inc(xtr_done, 1)

            def expert_of(n):
                if routed(n):
                    return pe.value_load(eid[0:1, bass.ds(n - SF, 1)], min_val=0, max_val=E - 1)
                return SH

            def up(n, u):
                e = expert_of(n)
                if routed(n):
                    pe.wait_ge(xT_ready, n - SF + 1)
                if not isinstance(n, int) or n >= 2:
                    pe.wait_ge(gated_ready, n - 1)
                for i in range(2):
                    for c in range(C):
                        if routed(n):
                            x = xT[:, u, c * P:(c + 1) * P]
                        else:
                            x = h1T[:, c, shared_tile(n) * P:(shared_tile(n) + 1) * P]
                        last = mm(ps_lo[:, u * 2 + i, 0:HID], x, w13[:, c, bass.ds(e * H2 + i * HID, HID)],
                                  start=(c == 0), stop=(c == C - 1))
                last.then_inc(mm1_done, 1)

            def hid_transpose(n, u):
                pe.wait_ge(hid_ready, n + 1)
                if not isinstance(n, int) or n >= 1:
                    pe.wait_ge(hidT_ready, n)
                for j, (s, m) in enumerate(HC):
                    last = nc.tensor.transpose(ps_hi[0:m, 1, j * P:(j + 1) * P], hid[:, u, s:s + m], ident[:, :])
                last.then_inc(htr_done, 1)

            def down(n, u):
                e = expert_of(n)
                pe.wait_ge(hidT_ready, n + 1)
                if not isinstance(n, int) or n >= 1:
                    pe.wait_ge(y_ready, n)
                for j, (s, m) in enumerate(HC):
                    last = mm(ps_hi[:, 3, 0:D], hidT[0:m, u, j, :], w2s[0:m, j, bass.ds(e * D, D)],
                              start=(j == 0), stop=(j == NHC - 1))
                last.then_inc(mm2_done, 1)

            def step(n, u):
                if not isinstance(n, int) or SF <= n + 1 < RL:
                    x_transpose(n + 1, 1 - u)
                if not isinstance(n, int) or n < NS:
                    up(n, u)
                if not isinstance(n, int) or 1 <= n <= NS:
                    hid_transpose(n - 1, 1 - u)
                if not isinstance(n, int) or n >= 2:
                    down(n - 2, u)

            def prefix():
                pe.wait_ge(sel_ready, 1)
                mm(ps_hi[:, 2, 0:NT * E], before[:, :], sel[:, :, :], start=True, stop=False)
                mm(ps_hi[:, 2, 0:NT * E], ones_bf[:, :], selcum[:, 0:NT, :], start=False, stop=True)
                mm(ps_hi[:, 2, NT * E:NT * E + E], ones_bf[:, :], selcum[:, NT, :], start=True,
                   stop=True).then_inc(prefix_done, 1)

            def slot_tokens():
                pe.wait_ge(onehot_ready, 1)
                for i in range(TOP * NT):
                    last = mm(ps_hi[:, 2, 0:2 * R], at_pos[:, i, :], ids[:, i, :], start=(i == 0),
                              stop=(i == TOP * NT - 1))
                last.then_inc(index_done, 1)

            pe.wait_ge(weights_loaded, 16 * 4 * NE)
            for n in range(LOOP0):
                if n == SF - 1:
                    pe.wait_ge(eid_ready, 1)
                step(n, n % 2)
                if n == 0:
                    prefix()
                if n == 1:
                    slot_tokens()
            with pe.Fori(LOOP0, LOOP1 - 1, 2) as n:
                step(n, 0)
                step(n + 1, 1)
            for n in range(LOOP1, NS + 2):
                step(n, n % 2)


_IN = ["patches_T", "tok_wT", "tok_b", "bq", "bk", "bv_row", "gate_wT", "gate_b", "w1", "b1", "w3", "b3",
       "w2", "b2", "sw1", "sb1", "sw3", "sb3", "sw2", "sb2"]


def kernel(**inputs):
    import numpy as np
    import concourse.bacc as bacc
    from concourse.bass_utils import run_bass_kernel_spmd

    a = {n.replace("L0_", ""): np.asarray(x) for n, x in inputs.items()}
    B, C, H, W = a["x"].shape
    PS = 16
    h, w = H // PS, W // PS
    D = a["tok_W"].shape[0]
    laid = {
        "patches_T": a["x"].reshape(B, C, h, PS, w, PS).transpose(1, 3, 5, 0, 2, 4).reshape(C * PS * PS, B * h * w),
        "tok_wT": a["tok_W"].T,
        "tok_b": a["tok_b"].reshape(D // P, P).T,
        "bq": a["attn_bv_q"].reshape(D // P, P).T,
        "bk": a["attn_bv_k"].reshape(D // P, P).T,
        "bv_row": a["attn_bv_v"].reshape(D),
        "gate_wT": a["ffn_gate_w"].T,
        **{n: a["ffn_" + n] for n in _IN[7:]},
    }
    nc = bacc.Bacc("TRN2", target_bir_lowering=False, num_devices=1)
    arrays, args = {}, []
    for n in _IN:
        x = np.ascontiguousarray(laid[n])
        arrays[f"in_{n}"] = x
        args.append(nc.dram_tensor(f"in_{n}", x.shape, mybir.dt.from_np(x.dtype), kind="ExternalInput").ap())
    out = nc.dram_tensor("out", (B * h * w, D), F32, kind="ExternalOutput").ap()
    vit_layer(nc, *args, out)
    r = run_bass_kernel_spmd(nc, [arrays], core_ids=[0])
    return r.results[0]["out"].reshape(B, h * w, D)
```

```python
from contextlib import ExitStack

import concourse.bass as bass
from concourse import mybir

F32 = mybir.dt.float32
BF16 = mybir.dt.bfloat16
I32 = mybir.dt.int32
ALU = mybir.AluOpType
ACT = mybir.ActivationFunctionType
AX = mybir.AxisListType

P = 128
EPS = 1e-5
MASKED = -1e30


def vit_layer(nc, patches_T, tok_wT, tok_b, bq, bk, bv_row, gate_wT, gate_b,
              w1, b1, w3, b3, w2, b2, sw1, sw3, sb13_T, sw2, sb2, out):
    K_IN, TOK = patches_T.shape
    D = tok_wT.shape[1]
    IMG = 36
    KC = K_IN // P
    C = D // P
    NH, HD = 16, 16
    HPC = P // HD
    GROUPS = P // 32
    BH = 4
    E, _, HID = w1.shape
    SH = E
    NE = E + 1
    TT = 3 * IMG
    NA = -(-TOK // TT)
    LAST = TOK - (NA - 1) * TT
    CH = 3 * TT
    CHUNKS = [(s, min(CH, TOK - s)) for s in range(0, TOK, CH)]
    NT = TOK // P
    TOP = 2
    DT = 4
    R = (TOP * TOK - E) // P + E
    H2 = 2 * HID
    GRP = 3
    GT = GRP * P
    HC = [(s, min(P, HID - s)) for s in range(0, HID, P)]
    NHC = len(HC)

    h1_dram = nc.dram_tensor("h1_rows", (TOK, D), F32).ap()
    y_dram = nc.dram_tensor("y_rows", (TOP * TOK + R * P, D), F32).ap()

    with ExitStack() as ctx:
        def sb(name, shape, dt=F32):
            return ctx.enter_context(nc.sbuf_tensor(name, shape, dt))

        def sem(name):
            return ctx.enter_context(nc.semaphore(name))

        ident = sb("ident", [P, P])
        ident_bf = sb("ident_bf", [P, P], BF16)
        zeros_tt = sb("zeros_tt", [TT, TT])
        mask_f = sb("mask_f", [TT, TT])
        mask_bf = sb("mask_bf", [TT, TT], BF16)
        before = sb("before", [P, P], BF16)
        ones_bf = sb("ones_bf", [P, P], BF16)
        ones_f = sb("ones_f", [P, P])
        part = sb("part", [P, 1], I32)
        part_f = sb("part_f", [P, 1])
        head_i = sb("head_i", [P, 1], I32)
        head_f = sb("head_f", [P, 1])
        own_head = sb("own_head", [P, HPC])
        iota_row = sb("iota_row", [P, P], I32)
        iota_f = sb("iota_f", [P, P])
        tri_i = sb("tri_i", [P, E, E])
        half_neg = sb("half_neg", [P, 1])
        eps = sb("eps", [P, 1])
        wT = sb("wT", [P, KC, D])
        bias_d = sb("bias_d", [P, C])
        qk = sb("qk", [P, 2, C])
        vrow = sb("vrow", [P, D])
        sgn = sb("sgn", [P, 6, C])
        sgn_qk = sb("sgn_qk", [P, C])
        sel_qk = sb("sel_qk", [P, C, HPC])
        vs = sb("vs", [P, 2, D])
        sgn_v = sb("sgn_v", [P, D])
        gwT = sb("gwT", [P, C, E])
        gb = sb("gb", [P, E])
        w13 = sb("w13", [P, C, NE * H2])
        w2s = sb("w2s", [P, NHC, NE * D])
        hT_acc = sb("hT_acc", [P, C * TOK])
        hT = hT_acc[:, :].rearrange("p (c t) -> p c t", c=C)
        acc = hT_acc[:, :].rearrange("p (t d) -> p t d", t=NT)
        htok = sb("htok", [P, NA, D])
        resid = htok
        h1T = sb("h1T", [P, C, TOK])
        gath = sb("gath", [P, KC * TOK])
        patch = gath[:, :].rearrange("p (k t) -> p k t", k=KC)
        xg = gath[:, 0:2 * D].rearrange("p (u d) -> p u d", u=2)
        hsT = gath[:, TOP * NT * D:TOP * NT * D + 2 * NHC * GT].rearrange("p (u m t) -> p u m t", u=2, m=NHC)
        yg = gath[:, 0:TOP * NT * D].rearrange("p (t k d) -> p t k d", t=NT, k=TOP)
        QN = C * HPC * TT
        AN = NH * TT
        VN = NH * 32
        BN = max(2 * (QN + AN + VN), E * H2 + NE * D)
        scratch = sb("scratch", [P, BN])
        sb13 = sb("sb13", [P, 2, NHC])
        qx = [scratch[:, i * QN:(i + 1) * QN].rearrange("p (c h t) -> p c h t", c=C, h=HPC) for i in range(2)]
        att = [scratch[:, 2 * QN + i * AN:2 * QN + (i + 1) * AN].rearrange("p (b x) -> p b x", b=NH // BH)
               for i in range(2)]
        vt = [scratch[:, 2 * (QN + AN) + i * VN:2 * (QN + AN) + (i + 1) * VN] for i in range(2)]
        b13 = scratch[:, 0:E * H2]
        b2b = scratch[:, E * H2:E * H2 + NE * D]
        zT = sb("zT", [P, 2, C * TT])
        stats = sb("stats", [P, 2, 6])
        mv = sb("mv", [P, 2, 2])
        var_eps = sb("var_eps", [P, 2, 1])
        rstd = sb("rstd", [P, 2, 1])
        stats2 = sb("stats2", [P, NT, 6])
        mv2 = sb("mv2", [P, NT, 2])
        var_eps2 = sb("var_eps2", [P, NT])
        rstd2 = sb("rstd2", [P, NT])
        route_at = [0]

        def route_f(n):
            route_at[0] += n
            return gath[:, route_at[0] - n:route_at[0]]

        lg = sb("lg", [P, NT, E])
        lmax = sb("lmax", [P, NT])
        lex = sb("lex", [P, NT, E])
        lsum = sb("lsum", [P, NT])
        lrec = sb("lrec", [P, NT])
        probs = sb("probs", [P, NT, E])
        biased = sb("biased", [P, NT, E])
        pair_a = route_f(NT * E * E).rearrange("p (t e j) -> p t e j", t=NT, e=E)
        pair_b = route_f(NT * E * E).rearrange("p (t e j) -> p t e j", t=NT, e=E)
        rank = sb("rank", [P, NT, E])
        hot = sb("hot", [P, TOP, NT, E])
        sel = sb("sel", [P, NT + 1, E], BF16)
        rw = sb("rw", [P, TOP, NT])
        tmp = sb("tmp", [P, TOP, NT, E])
        full = sb("full", [P, NT])
        cmp_n = sb("cmp_n", [P, E, NT])
        ntile = sb("ntile", [P, E])
        cmp_c = sb("cmp_c", [P, E, E])
        tstart = sb("tstart", [P, E])
        tend = sb("tend", [P, E])
        place = sb("place", [P, NT, E])
        slot_f = sb("slot_f", [P, TOP, NT])
        slot = sb("slot", [P, TOP * NT], I32)
        slot_hi = sb("slot_hi", [P, TOP * NT], I32)
        slot_lo = sb("slot_lo", [P, TOP * NT], I32)
        hi_f = sb("hi_f", [P, TOP * NT])
        lo_f = sb("lo_f", [P, TOP * NT])
        in_tile = route_f(TOP * NT * R).rearrange("p (i r) -> p i r", r=R)
        at_pos = route_f(TOP * NT * P // 2).bitcast(BF16).rearrange("p (i q) -> p i q", q=P)
        ids = route_f(TOP * NT * 2 * R).bitcast(BF16).rearrange("p (i r) -> p i r", r=4 * R)
        idx_f = sb("idx_f", [P, 4 * R])
        idx = sb("idx", [P, R], I32)
        spare = sb("spare", [P, R])
        dest_f = sb("dest_f", [P, R])
        dest = sb("dest", [P, R], I32)
        cmp_e = route_f(R * E).rearrange("p (r e) -> p r e", e=E)
        eid_f = sb("eid_f", [P, R])
        eid_c = sb("eid_c", [P, R])
        eid = sb("eid", [P, R], I32)
        diag = wT[:, :, :].rearrange("p k d -> p (k d)")[:, 0:(NT - DT) * TOP * P].rearrange(
            "p (t k q) -> p t k q", t=NT - DT, k=TOP)
        xT = sb("xT", [P, 2, C * P])
        work = sb("work", [P, 6 * HID])
        up1 = work[:, 0:HID]
        up3 = work[:, HID:2 * HID]
        gated = work[:, 2 * HID:4 * HID].rearrange("p (u n) -> p u n", u=2)
        hid = work[:, 4 * HID:6 * HID].rearrange("p (u n) -> p u n", u=2)
        sup1 = work[:, 0:2 * GT].rearrange("p (u t) -> p u t", u=2)
        sgated = work[:, 2 * GT:4 * GT].rearrange("p (u t) -> p u t", u=2)
        hidT = sb("hidT", [P, 2, NHC, P])
        yb = sb("yb", [P, 2, D])

        ps_lo = ctx.enter_context(nc.psum_tensor("ps_lo", [P, 4, 512], F32))
        ps_hi = ctx.enter_context(nc.psum_tensor("ps_hi", [P, 4, 512], F32))

        wT_loaded = sem("wT_loaded")
        small_loaded = sem("small_loaded")
        patch_loaded = [sem(f"patch_loaded{n}") for n in range(len(CHUNKS))]
        weights_loaded = sem("weights_loaded")
        sbias_loaded = sem("sbias_loaded")
        sb2_loaded = sem("sb2_loaded")
        rbias_loaded = sem("rbias_loaded")
        resid_loaded = sem("resid_loaded")
        pool_chain = sem("pool_chain")
        consts_ready = sem("consts_ready")
        dve_chain = sem("dve_chain")
        embed_done = sem("embed_done")
        hT_ready = sem("hT_ready")
        q_ready = sem("q_ready")
        scores_done = sem("scores_done")
        sig_done = sem("sig_done")
        tr_done = sem("tr_done")
        v_ready = sem("v_ready")
        av_done = sem("av_done")
        zT_ready = sem("zT_ready")
        ztr_done = sem("ztr_done")
        stats_ready = sem("stats_ready")
        mv_ready = sem("mv_ready")
        vareps_ready = sem("vareps_ready")
        rstd_ready = sem("rstd_ready")
        h1_ready = sem("h1_ready")
        h1_stored = sem("h1_stored")
        h1tr_done = sem("h1tr_done")
        h1T_ready = sem("h1T_ready")
        logits_done = sem("logits_done")
        shifted_ready = sem("shifted_ready")
        exp_done = sem("exp_done")
        sel_ready = sem("sel_ready")
        prefix_done = sem("prefix_done")
        in_tile_ready = sem("in_tile_ready")
        ids_ready = sem("ids_ready")
        at_pos_ready = sem("at_pos_ready")
        rw_ready = sem("rw_ready")
        diag_ready = sem("diag_ready")
        index_done = sem("index_done")
        eid_ready = sem("eid_ready")
        spare_ready = sem("spare_ready")
        idx_ready = sem("idx_ready")
        dest_ready = sem("dest_ready")
        xg_loaded = [sem(f"xg_loaded{i}") for i in range(2)]
        xtr_done = sem("xtr_done")
        xT_ready = sem("xT_ready")
        mm1_done = sem("mm1_done")
        sup_done = sem("sup_done")
        sup1_ready = sem("sup1_ready")
        sgated_ready = sem("sgated_ready")
        shid_ready = sem("shid_ready")
        up1_ready = sem("up1_ready")
        up3_ready = sem("up3_ready")
        gated_ready = sem("gated_ready")
        hid_ready = sem("hid_ready")
        htr_done = sem("htr_done")
        hidT_ready = sem("hidT_ready")
        mm2_done = sem("mm2_done")
        y_ready = sem("y_ready")
        resid_ready = sem("resid_ready")
        y_stored = [sem(f"y_stored{i}") for i in range(2)]
        yg_loaded = [sem(f"yg_loaded{i}") for i in range(NT)]
        mix0_ready = sem("mix0_ready")
        mix_ready = sem("mix_ready")
        sum_done = sem("sum_done")
        stats2_ready = sem("stats2_ready")
        mv2_ready = sem("mv2_ready")
        vareps2_ready = sem("vareps2_ready")
        rstd2_ready = sem("rstd2_ready")
        final_ready = sem("final_ready")
        out_stored = sem("out_stored")

        SF = 2 * GRP
        NS = NT + R
        BATCHES = [(0, DT), (DT, NT - 2), (NT - 2, NT)]
        LOOP0 = 4
        LOOP1 = R - 1

        def shared_place(t):
            return t if t < SF else t + R

        def bank_pair(i):
            return (i + i // (2 * NHC)) % 2

        def y_bank(t):
            return ps_hi[:, 0 if t % 2 == 1 and t != SF - 1 else 3, 0:D]

        def routed_y_bank(r):
            return ps_hi[:, 0 if isinstance(r, int) and r == R - 1 else 3, 0:D]

        def sum_of(t):
            if t < DT:
                return acc[:, t, :]
            banks = [ps_hi[:, 1], ps_hi[:, 2]] + [ps_lo[:, i] for i in range(4)]
            return banks[t - DT][:, 0:D]

        def small_inputs():
            return [(bias_d[:, :], tok_b), (qk[:, 0, :], bq), (qk[:, 1, :], bk),
                    (vrow[:, :], bv_row.partition_broadcast(P)),
                    (gwT[:, :, :], gate_wT.rearrange("(c p) e -> p c e", p=P)),
                    (gb[:, :], gate_b.partition_broadcast(P))]

        block = ctx.enter_context(nc.Block())

        @block.sync
        def _(sp):
            sp.dma_start(wT[:, :, :], tok_wT.rearrange("(k p) d -> p k d", p=P)).then_inc(wT_loaded, 16)
            for n, (s, m) in enumerate(CHUNKS):
                sp.dma_start(patch[:, :, s:s + m],
                             patches_T[:, s:s + m].rearrange("(k p) t -> p k t", p=P)).then_inc(patch_loaded[n], 16)
                if n == 0:
                    for dst, src in small_inputs():
                        sp.dma_start(dst, src).then_inc(small_loaded, 16)
            full_rows = (HID // P) * P
            sp.dma_start(sb13[:, :, :], sb13_T).then_inc(sbias_loaded, 16)
            for e, (a, c, d) in [(SH, (sw1, sw3, sw2))] + [(e, (w1[e], w3[e], w2[e])) for e in range(E)]:
                for i, w in enumerate((a, c)):
                    sp.dma_start(w13[:, :, e * H2 + i * HID:e * H2 + (i + 1) * HID],
                                 w.rearrange("(c p) n -> p c n", p=P)).then_inc(weights_loaded, 16)
                sp.dma_start(w2s[:, 0:HID // P, e * D:(e + 1) * D],
                             d[0:full_rows, :].rearrange("(c p) n -> p c n", p=P)).then_inc(weights_loaded, 16)
                sp.dma_start(w2s[0:HID - full_rows, NHC - 1, e * D:(e + 1) * D],
                             d[full_rows:HID, :]).then_inc(weights_loaded, 16)
            with sp.Fori(0, NA - 1) as t:
                sp.wait_ge(h1_ready, t + 1)
                sp.dma_start(h1_dram[bass.ds(t * TT, TT), :], htok[0:TT, bass.ds(t, 1), :]).then_inc(h1_stored, 16)
            sp.wait_ge(h1_ready, NA)
            sp.dma_start(h1_dram[(NA - 1) * TT:TOK, :], htok[0:LAST, NA - 1, :]).then_inc(h1_stored, 16)
            sp.wait_ge(av_done, NA)
            sp.dma_start(b2b[:, SH * D:(SH + 1) * D], sb2.partition_broadcast(P)).then_inc(sb2_loaded, 16)
            sp.wait_ge(h1_stored, 16 * NA)
            sp.wait_ge(h1tr_done, NA)
            sp.dma_start(resid[:, 0:NT, :], h1_dram.rearrange("(t p) d -> p t d", p=P)).then_inc(resid_loaded, 16)
            for i, b in enumerate((b1, b3)):
                sp.dma_start(b13[:, 0:E * H2].rearrange("p (e x) -> p e x", e=E)[:, :, i * HID:(i + 1) * HID],
                             b.partition_broadcast(P)).then_inc(rbias_loaded, 16)
            sp.dma_start(b2b[:, 0:E * D].rearrange("p (e x) -> p e x", e=E),
                         b2.partition_broadcast(P)).then_inc(rbias_loaded, 16)

            sp.wait_ge(y_stored[0], 16 * ((R + 1) // 2))
            sp.wait_ge(y_stored[1], 16 * (R // 2))
            for t in range(NT):
                sp.dma_start(yg[:, t, :, :], y_dram[TOP * t * P:TOP * (t + 1) * P, :].rearrange(
                    "(p k) d -> p k d", k=TOP)).then_inc(yg_loaded[t], 16)
            for a, b in BATCHES:
                sp.wait_ge(final_ready, b)
                sp.dma_start(out[a * P:b * P, :].rearrange("(t p) d -> p t d", p=P),
                             acc[:, a:b, :]).then_inc(out_stored, 16)
            sp.wait_ge(out_stored, 16 * len(BATCHES))

        @block.gpsimd
        def _(pool):
            chain = [0]

            def link(ins):
                chain[0] += 1
                ins.then_inc(pool_chain, 1)
                pool.wait_ge(pool_chain, chain[0])

            nc.gpsimd.memset(half_neg[:, :], -0.5)
            nc.gpsimd.memset(eps[:, :], EPS)
            nc.gpsimd.iota(part[:, :], [[0, 1]], base=0, channel_multiplier=1)
            nc.gpsimd.iota(iota_row[:, :], [[1, P]], base=0, channel_multiplier=0)
            nc.gpsimd.memset(zeros_tt[:, :], 0.0)
            link(nc.gpsimd.memset(ones_f[:, :], 1.0))
            nc.gpsimd.affine_select(out=ident[:, :], in_=ones_f[:, :], compare_op=ALU.is_equal, fill=0.0, base=0,
                                    pattern=[[-1, P]], channel_multiplier=1)
            nc.gpsimd.affine_select(out=before[:, :], in_=ones_f[:, :], compare_op=ALU.is_gt, fill=0.0, base=0,
                                    pattern=[[1, P]], channel_multiplier=-1)
            nc.gpsimd.affine_select(out=tri_i[:, :, :], in_=ones_f[:, 0:E * E].rearrange("p (e j) -> p e j", e=E),
                                    compare_op=ALU.is_gt, fill=0.0, base=0,
                                    pattern=[[1, E], [-1, E]], channel_multiplier=0)
            link(nc.gpsimd.affine_select(out=mask_f[:, :], in_=zeros_tt[:, :], compare_op=ALU.is_ge, fill=MASKED,
                                         base=0, pattern=[[1, TT]], channel_multiplier=-1))
            link(nc.gpsimd.affine_select(out=mask_bf[:, :].rearrange("p (a q) -> p a q", q=IMG),
                                         in_=mask_f[:, :].rearrange("p (a q) -> p a q", q=IMG),
                                         compare_op=ALU.is_ge, fill=MASKED, base=0,
                                         pattern=[[-IMG, TT // IMG], [0, IMG]], channel_multiplier=1))
            nc.gpsimd.tensor_copy(ident_bf[:, :], ident[:, :])
            nc.gpsimd.tensor_copy(ones_bf[:, :], ones_f[:, :])
            nc.gpsimd.tensor_copy(iota_f[:, :], iota_row[:, :])
            link(nc.gpsimd.tensor_copy(part_f[:, :], part[:, :]))
            nc.gpsimd.memset(sel[:, NT, :], 0.0).then_inc(consts_ready, 1)

            def inverse_deviation(t, u, rows):
                pool.wait_ge(mv_ready, t + 1)
                nc.gpsimd.tensor_tensor(var_eps[0:rows, u, :], mv[0:rows, u, 1:2], eps[0:rows, :],
                                        ALU.add).then_inc(vareps_ready, 1)
                pool.wait_ge(vareps_ready, t + 1)
                nc.gpsimd.tensor_tensor(rstd[0:rows, u, :], var_eps[0:rows, u, :], half_neg[0:rows, :],
                                        ALU.pow).then_inc(rstd_ready, 1)

            nc.gpsimd.iota(idx[:, :], [[P, R]], base=TOP * TOK, channel_multiplier=1).then_inc(pool_chain, 1)
            pool.wait_ge(pool_chain, chain[0] + 1)
            nc.gpsimd.tensor_copy(spare[:, :], idx[:, :]).then_inc(spare_ready, 1)
            with pool.Fori(0, NA - 2, 2) as t:
                inverse_deviation(t, 0, TT)
                inverse_deviation(t + 1, 1, TT)
            inverse_deviation(NA - 1, 0, LAST)

            pool.wait_ge(sb2_loaded, 16)
            pool.wait_ge(resid_loaded, 16)
            for g in range(NT // GRP):
                r = resid[:, g * GRP:(g + 1) * GRP, :]
                nc.gpsimd.tensor_tensor(r, r, b2b[:, SH * D:(SH + 1) * D].unsqueeze(1).broadcast_to([P, GRP, D]),
                                        ALU.add).then_inc(resid_ready, 1)

            def gather(r):
                if r >= 2:
                    pool.wait_ge(xg_loaded[r % 2], 16 * (r // 2))
                    pool.wait_ge(xtr_done, r - 1)
                nc.gpsimd.indirect_dma_start(
                    out=xg[:, r % 2, :], out_offset=None, in_=h1_dram,
                    in_offset=bass.IndirectOffsetOnAxis(ap=idx[:, r:r + 1], axis=0),
                ).then_inc(xg_loaded[r % 2], 16)

            def scatter(r):
                pool.wait_ge(y_ready, SF + r + 1)
                nc.gpsimd.indirect_dma_start(
                    out=y_dram, out_offset=bass.IndirectOffsetOnAxis(ap=dest[:, r:r + 1], axis=0),
                    in_=yb[:, r % 2, :], in_offset=None,
                ).then_inc(y_stored[r % 2], 16)

            nc.gpsimd.memset(ids[:, 0:NT, 2 * R:3 * R], 0.0)
            pool.wait_ge(in_tile_ready, 1)
            nc.gpsimd.tensor_tensor(ids[:, :, 0:R], in_tile[:, :, :],
                                    part_f[:, :].unsqueeze(1).broadcast_to([P, TOP * NT, R]), ALU.mult)
            for k in range(TOP):
                nc.gpsimd.tensor_tensor(ids[:, k * NT:(k + 1) * NT, R:2 * R], in_tile[:, k * NT:(k + 1) * NT, :],
                                        iota_f[:, 0:NT].unsqueeze(2).broadcast_to([P, NT, R]), ALU.mult)
            nc.gpsimd.tensor_copy(ids[:, NT:2 * NT, 2 * R:3 * R], in_tile[:, NT:2 * NT, :])
            nc.gpsimd.tensor_copy(ids[:, :, 3 * R:4 * R], in_tile[:, :, :]).then_inc(ids_ready, 1)
            pool.wait_ge(h1_stored, 16 * NA)
            pool.wait_ge(idx_ready, 1)
            LAG = 5
            for r in range(R + LAG):
                if r < R:
                    gather(r)
                if r == LAG:
                    pool.wait_ge(dest_ready, 1)
                if r >= LAG:
                    scatter(r - LAG)
            for i, (a, b) in enumerate(BATCHES):
                pool.wait_ge(mv2_ready, b)
                nc.gpsimd.tensor_tensor(var_eps2[:, a:b], mv2[:, a:b, 1], eps[:, :].broadcast_to([P, b - a]),
                                        ALU.add).then_inc(vareps2_ready, 1)
                pool.wait_ge(vareps2_ready, i + 1)
                nc.gpsimd.tensor_tensor(rstd2[:, a:b], var_eps2[:, a:b], half_neg[:, :].broadcast_to([P, b - a]),
                                        ALU.pow).then_inc(rstd2_ready, 1)

        @block.scalar
        def _(act):
            act.wait_ge(small_loaded, 16 * len(small_inputs()))
            for n, (s, m) in enumerate(CHUNKS):
                for c in range(C):
                    act.wait_ge(embed_done, C * n + c + 1)
                    nc.scalar.activation(hT[:, c, s:s + m], ps_hi[:, (n % 2) * C + c, 0:m], ACT.Identity,
                                         bias=bias_d[:, c:c + 1]).then_inc(hT_ready, 1)

            def sigmoid(t, u, rows):
                act.wait_ge(scores_done, t + 1)
                if not isinstance(t, int) or t >= 2:
                    act.wait_ge(av_done, t - 1)
                nc.scalar.activation(
                    att[u][0:rows, :, 0:BH * rows], ps_lo[0:rows, :, 0:BH * rows],
                    ACT.Sigmoid).then_inc(sig_done, 1)

            def keep_h1T(t, rows):
                act.wait_ge(h1tr_done, t + 1)
                nc.scalar.activation(h1T[:, :, bass.ds(t * TT, rows)],
                                     ps_hi[:, 3, 0:C * rows].rearrange("p (c t) -> p c t", c=C),
                                     ACT.Copy).then_inc(h1T_ready, 1)

            sigmoid(0, 0, TT)
            sigmoid(1, 1, TT)
            sigmoid(2, 0, TT)
            with act.Fori(2, NA - 4, 2) as t:
                sigmoid(t + 1, 1, TT)
                keep_h1T(t - 2, TT)
                sigmoid(t + 2, 0, TT)
                keep_h1T(t - 1, TT)
            sigmoid(NA - 2, 1, TT)
            keep_h1T(NA - 5, TT)
            sigmoid(NA - 1, 0, LAST)
            keep_h1T(NA - 4, TT)
            keep_h1T(NA - 3, TT)
            keep_h1T(NA - 2, TT)

            def shared_up1(i):
                rows, u, m = HC[i % NHC][1], bank_pair(i), i % NHC
                act.wait_ge(sup_done, i + 1)
                if i >= 2:
                    act.wait_ge(sgated_ready, i - 1)
                if i == 2 * NHC:
                    act.wait_ge(gated_ready, R)
                    act.wait_ge(hid_ready, R)
                nc.scalar.activation(sup1[0:rows, u, :], ps_lo[0:rows, 2 * u, 0:GT], ACT.Identity,
                                     bias=sb13[0:rows, 0, m:m + 1]).then_inc(sup1_ready, 1)

            def shared_silu(i):
                rows, u, g, m = HC[i % NHC][1], bank_pair(i), i // NHC, i % NHC
                act.wait_ge(sgated_ready, i + 1)
                if i == 2 * NHC:
                    act.wait_ge(mm2_done, GRP)
                nc.scalar.activation(hsT[0:rows, g % 2, m, :], sgated[0:rows, u, :],
                                     ACT.Silu).then_inc(shid_ready, 1)

            act.wait_ge(sbias_loaded, 16)
            shared_up1(0)
            keep_h1T(NA - 1, LAST)
            act.wait_ge(shifted_ready, 1)
            nc.scalar.activation(lex[:, :, :], lg[:, :, :], ACT.Exp).then_inc(exp_done, 1)
            shared_up1(1)
            shared_silu(0)
            shared_silu(1)
            for i in range(2, 2 * NHC):
                shared_up1(i)
                shared_silu(i)

            def keep_xT(r, u):
                act.wait_ge(xtr_done, r + 1)
                if not isinstance(r, int) or r >= 2:
                    act.wait_ge(mm1_done, r - 1)
                nc.scalar.activation(xT[:, u, :], ps_hi[:, 0, 0:C * P], ACT.Copy).then_inc(xT_ready, 1)

            def silu(r, u):
                act.wait_ge(gated_ready, r + 1)
                if not isinstance(r, int) or r >= 2:
                    act.wait_ge(htr_done, r - 1)
                nc.scalar.activation(hid[:, u, :], gated[:, u, :], ACT.Silu).then_inc(hid_ready, 1)

            def keep_hidT(r, u):
                act.wait_ge(htr_done, r + 1)
                if not isinstance(r, int) or r >= 2:
                    act.wait_ge(mm2_done, SF + r - 1)
                nc.scalar.activation(hidT[:, u, 0:NHC - 1, :], ps_hi[:, 1, 0:(NHC - 1) * P], ACT.Copy)
                rows = HC[-1][1]
                nc.scalar.activation(hidT[0:rows, u, NHC - 1, :], ps_hi[0:rows, 1, (NHC - 1) * P:NHC * P],
                                     ACT.Copy).then_inc(hidT_ready, 1)

            def step(r, u):
                if not isinstance(r, int) or r + 1 < R:
                    keep_xT(r + 1, 1 - u)
                if not isinstance(r, int) or r >= 1:
                    keep_hidT(r - 1, 1 - u)
                silu(r, u)

            act.wait_ge(rw_ready, 1)
            for t in range(DT, NT):
                for k in range(TOP):
                    nc.scalar.activation(diag[:, t - DT, k, :], ident[:, :], ACT.Copy,
                                         scale=rw[:, k, t:t + 1]).then_inc(diag_ready, 1)
            keep_xT(0, 0)
            for r in range(LOOP0):
                step(r, r % 2)
            with act.Fori(LOOP0, LOOP1 - 1, 2) as r:
                step(r, 0)
                step(r + 1, 1)
            for r in range(LOOP1, R):
                step(r, r % 2)
            shared_up1(2 * NHC)
            keep_hidT(R - 1, (R - 1) % 2)
            shared_silu(2 * NHC)
            for i in range(2 * NHC + 1, 3 * NHC):
                shared_up1(i)
                shared_silu(i)

        @block.vector
        def _(dve):
            chain = [0]

            def link(ins):
                chain[0] += 1
                ins.then_inc(dve_chain, 1)
                dve.wait_ge(dve_chain, chain[0])

            v = nc.vector
            dve.wait_ge(consts_ready, 1)
            link(v.tensor_scalar(head_i[:, :], part[:, :], 4, None, ALU.arith_shift_right))
            link(v.tensor_copy(head_f[:, :], head_i[:, :]))
            v.tensor_scalar(own_head[:, :], iota_f[:, 0:HPC], head_f[:, :], None, ALU.is_equal)
            v.tensor_scalar(full[:, :], iota_f[:, 0:NT], float(P), None, ALU.mult)
            dve.wait_ge(small_loaded, 16 * len(small_inputs()))
            for i in range(2):
                v.tensor_scalar(sgn[:, i, :], qk[:, i, :], 0.0, None, ALU.is_gt)
                v.tensor_scalar(sgn[:, 2 + i, :], qk[:, i, :], 0.0, None, ALU.is_lt)
            v.tensor_scalar(vs[:, 0, :], vrow[:, :], 0.0, None, ALU.is_gt)
            link(v.tensor_scalar(vs[:, 1, :], vrow[:, :], 0.0, None, ALU.is_lt))
            link(v.tensor_tensor(sgn[:, 4:6, :], sgn[:, 0:2, :], sgn[:, 2:4, :], ALU.subtract))
            link(v.tensor_tensor(sgn_v[:, :], vs[:, 0, :], vs[:, 1, :], ALU.subtract))
            link(v.tensor_tensor(sgn_qk[:, :], sgn[:, 4, :], sgn[:, 5, :], ALU.mult))
            for c in range(C):
                last = v.tensor_scalar(sel_qk[:, c, :], own_head[:, :], sgn_qk[:, c:c + 1], None, ALU.mult)
            link(last)

            def queries(t, u, rows):
                if not isinstance(t, int) or t >= 2:
                    dve.wait_ge(scores_done, t - 1)
                for c in range(C):
                    last = v.tensor_tensor(qx[u][:, c, :, 0:rows],
                                           hT[:, bass.ds(c, 1), bass.ds(t * TT, rows)].broadcast_to([P, HPC, rows]),
                                           sel_qk[:, c, :].unsqueeze(2).broadcast_to([P, HPC, rows]), ALU.mult)
                last.then_inc(q_ready, 1)

            def values(t, u, rows):
                dve.wait_ge(tr_done, t + 1)
                if not isinstance(t, int) or t >= 2:
                    dve.wait_ge(av_done, t - 1)
                heads = vt[u][0:rows, :].rearrange("p (h x) -> p h x", x=64)
                for j in range(2):
                    last = v.tensor_tensor(heads[:, :, 48 * j:48 * j + HD],
                                           ps_hi[0:rows, 2, 0:D].rearrange("p (h j x) -> p h j x", j=2, x=HD)[:, :, j, :],
                                           sgn_v[0:rows, :].rearrange("p (h j x) -> p h j x", j=2, x=HD)[:, :, j, :],
                                           ALU.mult)
                last.then_inc(v_ready, 1)

            def residual(t, u, rows):
                dve.wait_ge(av_done, t + 1)
                if not isinstance(t, int) or t >= 2:
                    dve.wait_ge(ztr_done, t - 1)
                v.tensor_tensor(zT[:, u, 0:C * rows].rearrange("p (c t) -> p c t", c=C),
                                ps_hi[:, 0, 0:C * rows].rearrange("p (c t) -> p c t", c=C),
                                hT[:, :, bass.ds(t * TT, rows)], ALU.add).then_inc(zT_ready, 1)

            def moments(t, u, rows):
                dve.wait_ge(ztr_done, t + 1)
                v.bn_stats(stats[0:rows, u, :], ps_hi[0:rows, 1, 0:D]).then_inc(stats_ready, 1)
                dve.wait_ge(consts_ready, 1)
                dve.wait_ge(stats_ready, t + 1)
                v.bn_aggr(mv[0:rows, u, :], stats[0:rows, u, :]).then_inc(mv_ready, 1)

            def normalise(t, u, rows):
                dve.wait_ge(rstd_ready, t + 1)
                v.tensor_scalar(htok[0:rows, bass.ds(t, 1), :], ps_hi[0:rows, 1, 0:D],
                                mv[0:rows, u, 0:1], rstd[0:rows, u, :], ALU.subtract,
                                ALU.mult).then_inc(h1_ready, 1)

            def tile(t, u, rows, next_rows, after_rows=TT):
                if after_rows:
                    queries(t + 2, u, after_rows)
                if next_rows:
                    values(t + 1, 1 - u, next_rows)
                if not isinstance(t, int) or t >= 1:
                    moments(t - 1, 1 - u, TT)
                residual(t, u, rows)
                if not isinstance(t, int) or t >= 1:
                    normalise(t - 1, 1 - u, TT)

            for i in range(2):
                link(v.memset(vt[i][:, :], 0.0))
            dve.wait_ge(hT_ready, C * len(CHUNKS))
            queries(0, 0, TT)
            queries(1, 1, TT)
            values(0, 0, TT)
            tile(0, 0, TT, TT)
            with dve.Fori(1, NA - 5, 2) as t:
                tile(t, 1, TT, TT)
                tile(t + 1, 0, TT, TT)
            tile(NA - 4, 1, TT, TT)
            tile(NA - 3, 0, TT, TT, LAST)
            tile(NA - 2, 1, TT, LAST, 0)
            tile(NA - 1, 0, LAST, 0, 0)
            moments(NA - 1, 0, LAST)
            normalise(NA - 1, 0, LAST)

            def softmax():
                dve.wait_ge(logits_done, 1)
                lgp = ps_hi[:, 2, D:D + NT * E].rearrange("p (t e) -> p t e", e=E)
                link(v.tensor_reduce(lmax[:, :], lgp, AX.X, ALU.max))
                v.tensor_tensor(lg[:, :, :], lgp, lmax[:, :].unsqueeze(2).broadcast_to([P, NT, E]),
                                ALU.subtract).then_inc(shifted_ready, 1)
                dve.wait_ge(exp_done, 1)
                link(v.tensor_reduce(lsum[:, :], lex[:, :, :], AX.X, ALU.add))
                link(v.reciprocal(lrec[:, :], lsum[:, :]))
                link(v.tensor_tensor(probs[:, :, :], lex[:, :, :], lrec[:, :].unsqueeze(2).broadcast_to([P, NT, E]),
                                     ALU.mult))
                link(v.tensor_tensor(biased[:, :, :], probs[:, :, :], gb[:, :].unsqueeze(1).broadcast_to([P, NT, E]),
                                     ALU.add))

            def compare():
                other = biased[:, :, :].unsqueeze(2).broadcast_to([P, NT, E, E])
                own = biased[:, :, :].unsqueeze(3).broadcast_to([P, NT, E, E])
                v.tensor_tensor(pair_a[:, :, :, :], other, own, ALU.is_gt)
                link(v.tensor_tensor(pair_b[:, :, :, :], other, own, ALU.is_equal))

            def select():
                link(v.tensor_tensor(pair_b[:, :, :, :], pair_b[:, :, :, :],
                                     tri_i[:, :, :].unsqueeze(1).broadcast_to([P, NT, E, E]), ALU.mult))
                link(v.tensor_tensor(pair_a[:, :, :, :], pair_a[:, :, :, :], pair_b[:, :, :, :], ALU.add))
                link(v.tensor_reduce(rank[:, :, :], pair_a[:, :, :, :], AX.X, ALU.add))
                v.tensor_scalar(sel[:, 0:NT, :], rank[:, :, :], float(TOP), None, ALU.is_lt).then_inc(sel_ready, 1)
                for k in range(TOP):
                    last = v.tensor_scalar(hot[:, k, :, :], rank[:, :, :], float(k), None, ALU.is_equal)
                link(last)
                link(v.tensor_tensor(tmp[:, :, :, :], hot[:, :, :, :],
                                     probs[:, :, :].unsqueeze(1).broadcast_to([P, TOP, NT, E]), ALU.mult))
                v.tensor_reduce(rw[:, :, :], tmp[:, :, :, :], AX.X, ALU.add).then_inc(rw_ready, 1)

            def gate(r, u):
                e = dve.value_load(eid[0:1, bass.ds(r, 1)], min_val=0, max_val=E - 1)
                dve.wait_ge(mm1_done, r + 1)
                if not isinstance(r, int) or r >= 1:
                    dve.wait_ge(gated_ready, r)
                for i, (dst, done) in enumerate(((up1, up1_ready), (up3, up3_ready))):
                    v.tensor_tensor(dst, ps_lo[:, u * 2 + i, 0:HID], b13[:, bass.ds(e * H2 + i * HID, HID)],
                                    ALU.add).then_inc(done, 1)
                dve.wait_ge(up1_ready, r + 1)
                dve.wait_ge(up3_ready, r + 1)
                if isinstance(r, int) and r == 0:
                    dve.wait_ge(shid_ready, 2 * NHC)
                if not isinstance(r, int) or r >= 2:
                    dve.wait_ge(hid_ready, r - 1)
                v.tensor_tensor(gated[:, u, :], up1, up3, ALU.mult).then_inc(gated_ready, 1)

            def keep_y(r, u):
                dve.wait_ge(mm2_done, SF + r + 1)
                e = dve.value_load(eid[0:1, bass.ds(r, 1)], min_val=0, max_val=E - 1)
                if not isinstance(r, int) or r >= 2:
                    dve.wait_ge(y_stored[u], r // 2 * 16 if isinstance(r, int) else (r - u) * 8)
                v.tensor_tensor(yb[:, u, :], routed_y_bank(r), b2b[:, bass.ds(e * D, D)],
                                ALU.add).then_inc(y_ready, 1)

            def shared_gate(i):
                rows, u, m = HC[i % NHC][1], bank_pair(i), i % NHC
                dve.wait_ge(sup1_ready, i + 1)
                if i >= 2:
                    dve.wait_ge(shid_ready, i - 1)
                if i == 2 * NHC:
                    dve.wait_ge(hid_ready, R)
                    dve.wait_ge(htr_done, R)
                v.scalar_tensor_tensor(out=sgated[0:rows, u, :], in0=ps_lo[0:rows, 2 * u + 1, 0:GT],
                                       scalar=sb13[0:rows, 1, m:m + 1], in1=sup1[0:rows, u, :],
                                       op0=ALU.add, op1=ALU.mult).then_inc(sgated_ready, 1)

            def keep_shared(t):
                dve.wait_ge(mm2_done, shared_place(t) + 1)
                dve.wait_ge(resid_ready, t // GRP + 1)
                v.tensor_tensor(acc[:, t, :], y_bank(t), resid[:, t, :], ALU.add).then_inc(y_ready, 1)

            def step(r, u):
                gate(r, u)
                if not isinstance(r, int) or r >= 2:
                    keep_y(r - 2, u)

            def find_slots():
                dve.wait_ge(prefix_done, 1)
                count = ps_hi[:, 2, NT * E:NT * E + E]
                link(v.tensor_tensor(cmp_n[:, :, :], count.unsqueeze(2).broadcast_to([P, E, NT]),
                                     full[:, :].unsqueeze(1).broadcast_to([P, E, NT]), ALU.is_gt))
                link(v.tensor_reduce(ntile[:, :], cmp_n[:, :, :], AX.X, ALU.add))
                link(v.tensor_tensor(cmp_c[:, :, :], ntile[:, :].unsqueeze(1).broadcast_to([P, E, E]),
                                     tri_i[:, :, :], ALU.mult))
                link(v.tensor_reduce(tstart[:, :], cmp_c[:, :, :], AX.X, ALU.add))
                link(v.tensor_tensor(tend[:, :], tstart[:, :], ntile[:, :], ALU.add))
                link(v.tensor_tensor(cmp_e[:, :, :], iota_f[:, 0:R].unsqueeze(2).broadcast_to([P, R, E]),
                                     tend[:, :].unsqueeze(1).broadcast_to([P, R, E]), ALU.is_ge))
                link(v.tensor_reduce(eid_f[:, :], cmp_e[:, :, :], AX.X, ALU.add))
                link(v.tensor_scalar(eid_c[:, :], eid_f[:, :], float(E - 1), None, ALU.min))
                v.tensor_copy(eid[:, :], eid_c[:, :]).then_inc(eid_ready, 1)

            def token_slots():
                dve.wait_ge(rw_ready, 1)
                link(v.tensor_scalar(tstart[:, :], tstart[:, :], float(P), None, ALU.mult))
                link(v.tensor_tensor(place[:, :, :], ps_hi[:, 2, 0:NT * E].rearrange("p (t e) -> p t e", e=E),
                                     tstart[:, :].unsqueeze(1).broadcast_to([P, NT, E]), ALU.add))
                link(v.tensor_tensor(tmp[:, :, :, :], hot[:, :, :, :],
                                     place[:, :, :].unsqueeze(1).broadcast_to([P, TOP, NT, E]), ALU.mult))
                link(v.tensor_reduce(slot_f[:, :, :], tmp[:, :, :, :], AX.X, ALU.add))
                link(v.tensor_copy(slot[:, :], slot_f[:, :, :].rearrange("p k t -> p (k t)")))
                v.tensor_scalar(slot_hi[:, :], slot[:, :], 7, None, ALU.arith_shift_right)
                link(v.tensor_scalar(slot_lo[:, :], slot[:, :], P - 1, None, ALU.bitwise_and))
                v.tensor_copy(hi_f[:, :], slot_hi[:, :])
                link(v.tensor_copy(lo_f[:, :], slot_lo[:, :]))
                v.tensor_tensor(in_tile[:, :, :], iota_f[:, 0:R].unsqueeze(1).broadcast_to([P, TOP * NT, R]),
                                hi_f[:, :].unsqueeze(2).broadcast_to([P, TOP * NT, R]),
                                ALU.is_equal).then_inc(in_tile_ready, 1)

            def positions(k):
                last = v.tensor_tensor(at_pos[:, k * NT:(k + 1) * NT, :],
                                       iota_f[:, :].unsqueeze(1).broadcast_to([P, NT, P]),
                                       lo_f[:, k * NT:(k + 1) * NT].unsqueeze(2).broadcast_to([P, NT, P]),
                                       ALU.is_equal)
                if k == TOP - 1:
                    last.then_inc(at_pos_ready, 1)

            def find_tokens():
                dve.wait_ge(index_done, 1)
                link(v.tensor_copy(idx_f[:, :], ps_hi[:, 2, 0:4 * R]))
                link(v.scalar_tensor_tensor(out=idx_f[:, 0:R], in0=idx_f[:, R:2 * R], scalar=float(P),
                                            in1=idx_f[:, 0:R], op0=ALU.mult, op1=ALU.add))
                dve.wait_ge(spare_ready, 1)
                v.tensor_copy(idx[:, :], idx_f[:, 0:R]).then_inc(idx_ready, 1)

            def find_rows():
                link(v.scalar_tensor_tensor(out=dest_f[:, :], in0=idx_f[:, 0:R], scalar=float(TOP),
                                            in1=idx_f[:, 2 * R:3 * R], op0=ALU.mult, op1=ALU.add))
                link(v.tensor_tensor(dest_f[:, :], dest_f[:, :], spare[:, :], ALU.subtract))
                link(v.tensor_tensor(dest_f[:, :], dest_f[:, :], idx_f[:, 3 * R:4 * R], ALU.mult))
                link(v.tensor_tensor(dest_f[:, :], dest_f[:, :], spare[:, :], ALU.add))
                v.tensor_copy(dest[:, :], dest_f[:, :]).then_inc(dest_ready, 1)

            dve.wait_ge(sbias_loaded, 16)
            shared_gate(0)
            softmax()
            shared_gate(1)
            compare()
            shared_gate(2)
            select()
            shared_gate(3)
            find_slots()
            keep_shared(0)
            token_slots()
            shared_gate(4)
            positions(0)
            keep_shared(1)
            positions(1)
            shared_gate(5)
            keep_shared(2)
            find_tokens()
            keep_shared(3)
            find_rows()
            keep_shared(4)
            dve.wait_ge(eid_ready, 1)
            dve.wait_ge(rbias_loaded, 16 * 3)
            step(0, 0)
            keep_shared(5)
            for r in range(1, LOOP0):
                step(r, r % 2)
            with dve.Fori(LOOP0, LOOP1 - 1, 2) as r:
                step(r, 0)
                step(r + 1, 1)
            for r in range(LOOP1, R):
                step(r, r % 2)
            keep_y(R - 2, (R - 2) % 2)
            shared_gate(6)
            keep_y(R - 1, (R - 1) % 2)
            shared_gate(7)
            shared_gate(8)

            def combine(t):
                dve.wait_ge(yg_loaded[t], 16)
                dve.wait_ge(y_ready, shared_place(t) + 1)
                for k, done in enumerate((mix0_ready, mix_ready)):
                    v.scalar_tensor_tensor(out=acc[:, t, :], in0=yg[:, t, k, :], scalar=rw[:, k, t:t + 1],
                                           in1=acc[:, t, :], op0=ALU.mult, op1=ALU.add).then_inc(done, 1)
                    dve.wait_ge(done, t + 1)

            def moments2(t):
                if t >= DT:
                    dve.wait_ge(sum_done, t - DT + 1)
                v.bn_stats(stats2[:, t, :], sum_of(t)).then_inc(stats2_ready, 1)
                dve.wait_ge(stats2_ready, t + 1)
                v.bn_aggr(mv2[:, t, :], stats2[:, t, :]).then_inc(mv2_ready, 1)

            def finish(i):
                dve.wait_ge(rstd2_ready, i + 1)
                for t in range(*BATCHES[i]):
                    v.tensor_scalar(acc[:, t, :], sum_of(t), mv2[:, t, 0:1], rstd2[:, t:t + 1],
                                    ALU.subtract, ALU.mult).then_inc(final_ready, 1)

            for t in range(DT):
                combine(t)
                moments2(t)
                if t < NT - SF:
                    keep_shared(SF + t)
            moments2(DT)
            moments2(DT + 1)
            finish(0)
            moments2(DT + 2)
            moments2(DT + 3)
            moments2(DT + 4)
            finish(1)
            finish(2)

        @block.tensor
        def _(pe):
            mm = nc.tensor.matmul
            pe.wait_ge(wT_loaded, 16)
            for n, (s, m) in enumerate(CHUNKS):
                pe.wait_ge(patch_loaded[n], 16)
                if n >= 2:
                    pe.wait_ge(hT_ready, C * (n - 1))
                for c in range(C):
                    for k in range(KC):
                        last = mm(ps_hi[:, (n % 2) * C + c, 0:m], wT[:, k, c * P:(c + 1) * P], patch[:, k, s:s + m],
                                  start=(k == 0), stop=(k == KC - 1))
                    last.then_inc(embed_done, 1)

            def scores(t, rows):
                if not isinstance(t, int) or t >= 1:
                    pe.wait_ge(sig_done, t)
                pe.wait_ge(q_ready, t + 1)
                for b in range(NH // BH):
                    c, h = b * BH // HPC, b * BH % HPC
                    bank = ps_lo[0:rows, b, 0:BH * rows].rearrange("p (h q) -> p h q", h=BH)
                    mm(bank, ident_bf[0:rows, 0:rows],
                       mask_bf[0:rows, 0:rows].unsqueeze(1).broadcast_to([rows, BH, rows]), start=True, stop=False)
                    last = mm(bank, hT[:, c, t * TT:t * TT + rows], qx[t % 2][:, c, h:h + BH, 0:rows],
                              start=False, stop=True)
                last.then_inc(scores_done, 1)

            def to_tokens(t, rows):
                if t >= 1:
                    pe.wait_ge(v_ready, t)
                for c in range(C):
                    last = nc.tensor.transpose(ps_hi[0:rows, 2, c * P:(c + 1) * P], hT[:, c, bass.ds(t * TT, rows)],
                                               ident[:, :])
                last.then_inc(tr_done, 1)

            def attend(t, u, rows):
                pe.wait_ge(sig_done, t + 1)
                pe.wait_ge(v_ready, t + 1)
                if t >= 1:
                    pe.wait_ge(zT_ready, t)
                for c in range(C):
                    for j in range(2):
                        for g in range(GROUPS):
                            h = (c * GROUPS + g) * 2 + j
                            x = h % BH * rows
                            last = mm(ps_hi[32 * g:32 * g + 32, 0, c * rows:(c + 1) * rows],
                                      vt[u][0:rows, h * 32:(h + 1) * 32], att[u][0:rows, h // BH, x:x + rows],
                                      start=(j == 0), stop=(j == 1))
                last.then_inc(av_done, 1)

            def z_transpose(t, u, rows):
                pe.wait_ge(zT_ready, t + 1)
                if t >= 1:
                    pe.wait_ge(h1_ready, t)
                for c in range(C):
                    last = nc.tensor.transpose(ps_hi[0:rows, 1, c * P:(c + 1) * P],
                                               zT[:, u, c * rows:(c + 1) * rows], ident[:, :])
                last.then_inc(ztr_done, 1)

            def h1_transpose(t, rows):
                pe.wait_ge(h1_ready, t + 1)
                if not isinstance(t, int) or t >= 1:
                    pe.wait_ge(h1T_ready, t)
                for c in range(C):
                    last = nc.tensor.transpose(ps_hi[:, 3, c * rows:(c + 1) * rows],
                                               htok[0:rows, bass.ds(t, 1), c * P:(c + 1) * P], ident[0:rows, 0:rows])
                last.then_inc(h1tr_done, 1)

            def logits(t):
                pe.wait_ge(h1T_ready, t + 1)
                lo, hi = t * TT // P, (TOK if t == NA - 1 else (t + 1) * TT) // P
                for k in range(lo, hi):
                    for c in range(C):
                        last = mm(ps_hi[:, 2, D + k * E:D + (k + 1) * E], h1T[:, c, k * P:(k + 1) * P], gwT[:, c, :],
                                  start=(c == 0), stop=(c == C - 1))
                if t == NA - 1:
                    last.then_inc(logits_done, 1)

            def x_transpose(r, u):
                if isinstance(r, int) and r == 0:
                    pe.wait_ge(y_ready, SF - 2)
                pe.wait_ge(xg_loaded[u], 16 * (r // 2 + 1) if isinstance(r, int) else (r - u + 2) * 8)
                if not isinstance(r, int) or r >= 1:
                    pe.wait_ge(xT_ready, r)
                for c in range(C):
                    last = nc.tensor.transpose(ps_hi[:, 0, c * P:(c + 1) * P],
                                               xg[:, u, c * P:(c + 1) * P], ident[:, :])
                last.then_inc(xtr_done, 1)

            def up(r, u):
                e = pe.value_load(eid[0:1, bass.ds(r, 1)], min_val=0, max_val=E - 1)
                pe.wait_ge(xT_ready, r + 1)
                if isinstance(r, int) and r < 2:
                    pe.wait_ge(sgated_ready, 2 * NHC - 1 + r)
                else:
                    pe.wait_ge(gated_ready, r - 1)
                for i in range(2):
                    for c in range(C):
                        last = mm(ps_lo[:, u * 2 + i, 0:HID], xT[:, u, c * P:(c + 1) * P],
                                  w13[:, c, bass.ds(e * H2 + i * HID, HID)], start=(c == 0), stop=(c == C - 1))
                last.then_inc(mm1_done, 1)

            def hid_transpose(r, u):
                pe.wait_ge(hid_ready, r + 1)
                if not isinstance(r, int) or r >= 1:
                    pe.wait_ge(hidT_ready, r)
                for j, (s, m) in enumerate(HC):
                    last = nc.tensor.transpose(ps_hi[0:m, 1, j * P:(j + 1) * P], hid[:, u, s:s + m], ident[:, :])
                last.then_inc(htr_done, 1)

            def down(r, u):
                e = pe.value_load(eid[0:1, bass.ds(r, 1)], min_val=0, max_val=E - 1)
                pe.wait_ge(hidT_ready, r + 1)
                if isinstance(r, int) and r == R - 1:
                    pe.wait_ge(xT_ready, R)
                else:
                    pe.wait_ge(y_ready, SF + r)
                for j, (s, m) in enumerate(HC):
                    last = mm(routed_y_bank(r), hidT[0:m, u, j, :], w2s[0:m, j, bass.ds(e * D, D)],
                              start=(j == 0), stop=(j == NHC - 1))
                last.then_inc(mm2_done, 1)

            def step(r, u):
                up(r, u)
                if not isinstance(r, int) or r + 1 < R:
                    x_transpose(r + 1, 1 - u)
                if not isinstance(r, int) or r >= 1:
                    hid_transpose(r - 1, 1 - u)
                if not isinstance(r, int) or r >= 2:
                    down(r - 2, u)

            def shared_up(i):
                g, m, u = i // NHC, i % NHC, bank_pair(i)
                s, rows = HC[m]
                if i < 2:
                    pe.wait_ge(sig_done, NA)
                elif i == 2 * NHC:
                    pe.wait_ge(gated_ready, R - 1)
                elif i == 2 * NHC + 1:
                    pe.wait_ge(gated_ready, R)
                else:
                    pe.wait_ge(sgated_ready, i - 1)
                for j in range(2):
                    at = SH * H2 + j * HID + s
                    for c in range(C):
                        last = mm(ps_lo[0:rows, 2 * u + j, 0:GT], w13[:, c, at:at + rows],
                                  h1T[:, c, g * GT:(g + 1) * GT], start=(c == 0), stop=(c == C - 1))
                last.then_inc(sup_done, 1)

            def shared_down(t):
                g, x = t // GRP, t % GRP * P
                pe.wait_ge(shid_ready, NHC * (g + 1))
                if t == 0:
                    pe.wait_ge(h1T_ready, NA)
                elif t == 1:
                    pe.wait_ge(zT_ready, NA)
                elif t in (SF, SF + 1):
                    pe.wait_ge(xT_ready, R)
                    pe.wait_ge(y_ready, SF + R)
                elif t == SF - 1:
                    pe.wait_ge(y_ready, shared_place(t))
                else:
                    pe.wait_ge(y_ready, shared_place(t) - 1)
                for j, (s, m) in enumerate(HC):
                    last = mm(y_bank(t), hsT[0:m, g % 2, j, x:x + P], w2s[0:m, j, SH * D:(SH + 1) * D],
                              start=(j == 0), stop=(j == NHC - 1))
                last.then_inc(mm2_done, 1)

            def prefix():
                pe.wait_ge(sel_ready, 1)
                mm(ps_hi[:, 2, 0:(NT + 1) * E], before[:, :], sel[:, :, :], start=True, stop=False)
                for t in range(NT):
                    last = mm(ps_hi[:, 2, (t + 1) * E:(NT + 1) * E].rearrange("p (t e) -> p t e", e=E), ones_bf[:, :],
                              sel[:, t, :].unsqueeze(1).broadcast_to([P, NT - t, E]), start=False, stop=(t == NT - 1))
                last.then_inc(prefix_done, 1)

            def slot_tokens():
                pe.wait_ge(at_pos_ready, 1)
                pe.wait_ge(ids_ready, 1)
                for i in range(TOP * NT):
                    last = mm(ps_hi[:, 2, 0:4 * R], at_pos[:, i, :], ids[:, i, :], start=(i == 0),
                              stop=(i == TOP * NT - 1))
                last.then_inc(index_done, 1)

            pe.wait_ge(consts_ready, 1)
            pe.wait_ge(hT_ready, C * len(CHUNKS))
            rows = [TT] * (NA - 1) + [LAST]
            scores(0, TT)
            to_tokens(0, TT)
            for t in range(NA):
                if t + 1 < NA:
                    scores(t + 1, rows[t + 1])
                    if t >= 3:
                        pe.wait_ge(v_ready, t + 1)
                        logits(t - 3)
                    to_tokens(t + 1, rows[t + 1])
                if t >= 1:
                    z_transpose(t - 1, (t - 1) % 2, TT)
                attend(t, t % 2, rows[t])
                if t >= 2:
                    h1_transpose(t - 2, TT)
            z_transpose(NA - 1, (NA - 1) % 2, LAST)
            h1_transpose(NA - 2, TT)
            pe.wait_ge(weights_loaded, 16 * 4 * NE)
            shared_up(0)
            h1_transpose(NA - 1, LAST)
            pe.wait_ge(v_ready, NA)
            for t in range(NA - 4, NA):
                logits(t)
            shared_up(1)
            shared_up(2)
            shared_up(3)
            prefix()
            shared_down(0)
            shared_up(4)
            shared_down(1)
            shared_up(5)
            shared_down(2)
            slot_tokens()
            shared_down(3)
            shared_down(4)
            pe.wait_ge(eid_ready, 1)
            x_transpose(0, 0)
            up(0, 0)
            shared_down(5)
            x_transpose(1, 1)
            up(1, 1)
            x_transpose(2, 0)
            hid_transpose(0, 0)
            for r in range(2, LOOP0):
                step(r, r % 2)
            with pe.Fori(LOOP0, LOOP1 - 1, 2) as r:
                step(r, 0)
                step(r + 1, 1)
            for r in range(LOOP1, R):
                step(r, r % 2)
            shared_up(2 * NHC)
            hid_transpose(R - 1, (R - 1) % 2)
            down(R - 2, (R - 2) % 2)
            down(R - 1, (R - 1) % 2)
            shared_up(2 * NHC + 1)
            shared_up(2 * NHC + 2)

            def begin_sum(t):
                pe.wait_ge(y_ready, shared_place(t) + 1)
                mm(sum_of(t), ident[:, :], acc[:, t, :], start=True, stop=False)

            def end_sum(t):
                pe.wait_ge(yg_loaded[t], 16)
                for k in range(TOP):
                    last = mm(sum_of(t), diag[:, t - DT, k, :], yg[:, t, k, :], start=False, stop=(k == TOP - 1))
                last.then_inc(sum_done, 1)

            pe.wait_ge(diag_ready, TOP * (NT - DT))
            begin_sum(DT)
            begin_sum(DT + 1)
            shared_down(SF)
            shared_down(SF + 1)
            shared_down(SF + 2)
            end_sum(DT)
            pe.wait_ge(sgated_ready, 3 * NHC)
            begin_sum(DT + 2)
            begin_sum(DT + 3)
            end_sum(DT + 1)
            end_sum(DT + 2)
            begin_sum(DT + 4)
            end_sum(DT + 3)
            end_sum(DT + 4)


_IN = ["patches_T", "tok_wT", "tok_b", "bq", "bk", "bv_row", "gate_wT", "gate_b", "w1", "b1", "w3", "b3",
       "w2", "b2", "sw1", "sw3", "sb13_T", "sw2", "sb2"]


def kernel(**inputs):
    import numpy as np
    import concourse.bacc as bacc
    from concourse.bass_utils import run_bass_kernel_spmd

    a = {n.replace("L0_", ""): np.asarray(x) for n, x in inputs.items()}
    B, C, H, W = a["x"].shape
    PS = 16
    h, w = H // PS, W // PS
    D = a["tok_W"].shape[0]
    laid = {
        "patches_T": a["x"].reshape(B, C, h, PS, w, PS).transpose(1, 3, 5, 0, 2, 4).reshape(C * PS * PS, B * h * w),
        "tok_wT": a["tok_W"].T,
        "tok_b": a["tok_b"].reshape(D // P, P).T,
        "bq": a["attn_bv_q"].reshape(D // P, P).T,
        "bk": a["attn_bv_k"].reshape(D // P, P).T,
        "bv_row": a["attn_bv_v"].reshape(D),
        "gate_wT": a["ffn_gate_w"].T,
        "sb13_T": np.stack([np.pad(a["ffn_" + n], (0, -len(a["ffn_" + n]) % P)).reshape(-1, P).T
                            for n in ("sb1", "sb3")], axis=1),
        **{n: a["ffn_" + n] for n in _IN[7:] if n != "sb13_T"},
    }
    nc = bacc.Bacc("TRN2", target_bir_lowering=False, num_devices=1)
    arrays, args = {}, []
    for n in _IN:
        x = np.ascontiguousarray(laid[n])
        arrays[f"in_{n}"] = x
        args.append(nc.dram_tensor(f"in_{n}", x.shape, mybir.dt.from_np(x.dtype), kind="ExternalInput").ap())
    out = nc.dram_tensor("out", (B * h * w, D), F32, kind="ExternalOutput").ap()
    vit_layer(nc, *args, out)
    r = run_bass_kernel_spmd(nc, [arrays], core_ids=[0])
    return r.results[0]["out"].reshape(B, h * w, D)
```

```python
from contextlib import ExitStack

import concourse.bass as bass
from concourse import mybir

F32 = mybir.dt.float32
BF16 = mybir.dt.bfloat16
F32R = mybir.dt.float32r
I32 = mybir.dt.int32
ALU = mybir.AluOpType
ACT = mybir.ActivationFunctionType
AX = mybir.AxisListType

P = 128
EPS = 1e-5
MASKED = -1e30


def vit_layer(nc, patches_T, tok_wT, tok_b, bq, bk, bv_row, gate_wT, gate_b,
              w1, b1, w3, b3, w2, b2, sw1, sw3, sb13_T, sw2, sb2, out):
    K_IN, TOK = patches_T.shape
    D = tok_wT.shape[1]
    IMG = 36
    KC = K_IN // P
    C = D // P
    NH, HD = 16, 16
    HPC = P // HD
    GROUPS = P // 32
    E, _, HID = w1.shape
    SH = E
    NE = E + 1
    TI = 2
    TT = TI * IMG
    PL = P // TI
    NA = TOK // TT
    CH = 8 * IMG
    CHUNKS = [(s, min(CH, TOK - s)) for s in range(0, TOK, CH)]
    SLICES = [(0, 1), (1, KC // 2), (KC // 2, KC)]
    HALVES = [(0, KC // 2), (KC // 2, KC)]
    NT = TOK // P
    TOP = 2
    DT = 3
    R = (TOP * TOK - E) // P + E
    BATCHES = [(0, DT), (DT, NT - 3), (NT - 3, NT)]
    H2 = 2 * HID
    GRP = 3
    GT = GRP * P
    HC = [(s, min(P, HID - s)) for s in range(0, HID, P)]
    NHC = len(HC)

    h1_dram = nc.dram_tensor("h1_rows", (TOK, D), F32).ap()
    y_dram = nc.dram_tensor("y_rows", (TOP * TOK + R * P, D), F32).ap()

    with ExitStack() as ctx:
        def sb(name, shape, dt=F32):
            return ctx.enter_context(nc.sbuf_tensor(name, shape, dt))

        def sem(name):
            return ctx.enter_context(nc.semaphore(name))

        with ExitStack() as early:
            def split(name, width):
                return early.enter_context(nc.sbuf_tensor(name, [P, KC, width], F32R))

            w_hi, w_lo = split("w_hi", D), split("w_lo", D)
            patch_hi = [split(f"patch_hi{i}", CH) for i in range(2)]
            patch_lo = [split(f"patch_lo{i}", CH) for i in range(2)]

        htok = sb("htok", [P, NA, D])
        h1T = sb("h1T", [P, C, TOK])
        lex = sb("lex", [P, NT, E])
        probs = sb("probs", [P, NT, E])
        biased = sb("biased", [P, NT, E])
        rank = sb("rank", [P, NT, E])
        hot = sb("hot", [P, TOP, NT, E])
        tmp = sb("tmp", [P, TOP, NT, E])
        place = sb("place", [P, NT, E])
        xT = sb("xT", [P, 2, C * P])
        work = sb("work", [P, 6 * HID])
        hidT = sb("hidT", [P, 2, NHC, P])
        yb = sb("yb", [P, 2, D])

        ident = sb("ident", [P, P])
        ident_bf = sb("ident_bf", [P, P], BF16)
        zeros = sb("zeros", [P, IMG])
        mask_bf = sb("mask_bf", [P, IMG], BF16)
        before = sb("before", [P, P], BF16)
        ones_bf = sb("ones_bf", [P, P], BF16)
        ones_f = sb("ones_f", [P, P])
        part = sb("part", [P, 1], I32)
        part_f = sb("part_f", [P, 1])
        head_i = sb("head_i", [P, 1], I32)
        head_f = sb("head_f", [P, 1])
        own_head = sb("own_head", [P, HPC])
        iota_row = sb("iota_row", [P, P], I32)
        iota_f = sb("iota_f", [P, P])
        iota_b = sb("iota_b", [P, P], BF16)
        tri_i = sb("tri_i", [P, E, E])
        half_neg = sb("half_neg", [P, 1])
        eps = sb("eps", [P, 1])
        neg_one = sb("neg_one", [P, 1])
        wT = sb("wT", [P, KC, D])
        bias_d = sb("bias_d", [P, C])
        qk = sb("qk", [P, 2, C])
        sgn = sb("sgn", [P, 6, C])
        sgn_qk = sb("sgn_qk", [P, C])
        sel_qk = sb("sel_qk", [P, C, HPC])
        gwT = sb("gwT", [P, C, E])
        gb = sb("gb", [P, E])
        w13 = sb("w13", [P, C, NE * H2])
        w2s = sb("w2s", [P, NHC, NE * D])
        hT_acc = sb("hT_acc", [P, C * TOK // IMG * PL])
        hT = hT_acc[:, :].rearrange("p (c t) -> p c t", c=C)
        hT_images = hT_acc[:, :].rearrange("p (c i s) -> p c i s", c=C, s=PL)
        acc = hT_acc[:, 0:NT * D].rearrange("p (t d) -> p t d", t=NT)
        resid = htok
        gath = sb("gath", [P, KC * TOK])
        patch = gath[:, :].rearrange("p (k t) -> p k t", k=KC)
        xg = gath[:, 0:2 * D].rearrange("p (u d) -> p u d", u=2)
        hsT = gath[:, TOP * NT * D:TOP * NT * D + 2 * NHC * GT].rearrange("p (u m t) -> p u m t", u=2, m=NHC)
        yg = gath[:, 0:TOP * NT * D].rearrange("p (t k d) -> p t k d", t=NT, k=TOP)
        QN = C * HPC * TT
        AN = NH * TT
        VN = NH * 32
        BN = max(2 * (QN + AN + VN), E * H2 + NE * D)
        scratch = sb("scratch", [P, BN])
        sb13 = sb("sb13", [P, 2, NHC])
        qx = [scratch[:, i * QN:(i + 1) * QN].rearrange("p (c h t) -> p c h t", c=C, h=HPC) for i in range(2)]
        att = [scratch[:, 2 * QN + i * AN:2 * QN + (i + 1) * AN].rearrange("p (h t) -> p h t", h=NH) for i in range(2)]
        vt = [scratch[:, 2 * (QN + AN) + i * VN:2 * (QN + AN) + (i + 1) * VN] for i in range(2)]
        spare_at = 2 * (QN + AN + VN)
        vrow = scratch[:, spare_at:spare_at + D]
        vs = scratch[:, spare_at + D:spare_at + 3 * D].rearrange("p (i d) -> p i d", i=2)
        sgn_v = scratch[:, spare_at + 3 * D:spare_at + 4 * D]
        zT = scratch[:, spare_at + 4 * D:spare_at + 4 * D + 2 * C * TT].rearrange("p (u x) -> p u x", u=2)
        b13 = scratch[:, 0:E * H2]
        b2b = scratch[:, E * H2:E * H2 + NE * D]
        stats = sb("stats", [P, 2, 6])
        mv = sb("mv", [P, 2, 2])
        var_eps = sb("var_eps", [P, 2, 1])
        rstd = sb("rstd", [P, 2, 1])
        stats2 = sb("stats2", [P, NT, 6])
        mv2 = sb("mv2", [P, NT, 2])
        var_eps2 = sb("var_eps2", [P, NT])
        rstd2 = sb("rstd2", [P, NT])
        nmr2 = sb("nmr2", [P, NT])
        route_at = [0]

        def route_f(n):
            route_at[0] += n
            return gath[:, route_at[0] - n:route_at[0]]

        lg = sb("lg", [P, NT, E])
        lmax = sb("lmax", [P, NT])
        lsum = sb("lsum", [P, NT])
        lrec = sb("lrec", [P, NT])
        pair_a = route_f(NT * E * E).rearrange("p (t e j) -> p t e j", t=NT, e=E)
        pair_b = route_f(NT * E * E).rearrange("p (t e j) -> p t e j", t=NT, e=E)
        sel = sb("sel", [P, NT + 1, E], BF16)
        rw = sb("rw", [P, TOP, NT])
        full = sb("full", [P, NT])
        cmp_n = sb("cmp_n", [P, E, NT])
        ntile = sb("ntile", [P, E])
        cmp_c = sb("cmp_c", [P, E, E])
        tstart = sb("tstart", [P, E])
        sstart = sb("sstart", [P, E])
        tend = sb("tend", [P, E])
        slot_f = sb("slot_f", [P, TOP, NT])
        slot = sb("slot", [P, TOP * NT], I32)
        slot_hi = sb("slot_hi", [P, TOP * NT], I32)
        slot_lo = sb("slot_lo", [P, TOP * NT], I32)
        hi_b = sb("hi_b", [P, TOP * NT], BF16)
        lo_b = sb("lo_b", [P, TOP * NT], BF16)
        at_pos = route_f(TOP * NT * P // 2).bitcast(BF16).rearrange("p (i q) -> p i q", q=P)
        ids = route_f(TOP * NT * 2 * R).bitcast(BF16).rearrange("p (i r) -> p i r", r=4 * R)
        in_tile = ids[:, :, 3 * R:4 * R]
        idx_f = sb("idx_f", [P, 4 * R])
        idx = sb("idx", [P, R], I32)
        spare = sb("spare", [P, R])
        dest_f = sb("dest_f", [P, R])
        dest = sb("dest", [P, R], I32)
        cmp_e = route_f(R * E).rearrange("p (r e) -> p r e", e=E)
        eid_f = sb("eid_f", [P, R])
        eid_c = sb("eid_c", [P, R])
        eid = sb("eid", [P, R], I32)
        diag = wT[:, :, :].rearrange("p k d -> p (k d)")[:, 0:(NT - DT) * TOP * P].rearrange(
            "p (t k q) -> p t k q", t=NT - DT, k=TOP)
        up1 = work[:, 0:HID]
        up3 = work[:, HID:2 * HID]
        gated = work[:, 2 * HID:4 * HID].rearrange("p (u n) -> p u n", u=2)
        hid = work[:, 4 * HID:6 * HID].rearrange("p (u n) -> p u n", u=2)
        sup1 = work[:, 0:2 * GT].rearrange("p (u t) -> p u t", u=2)
        sgated = work[:, 2 * GT:4 * GT].rearrange("p (u t) -> p u t", u=2)

        ps_lo = ctx.enter_context(nc.psum_tensor("ps_lo", [P, 4, 512], F32))
        ps_hi = ctx.enter_context(nc.psum_tensor("ps_hi", [P, 4, 512], F32))

        slice_loaded = [sem(f"slice_loaded{i}") for i in range(len(SLICES))]
        small_loaded = sem("small_loaded")
        patch_loaded = [sem(f"patch_loaded{n}") for n in range(len(CHUNKS))]
        weights_loaded = sem("weights_loaded")
        sbias_loaded = sem("sbias_loaded")
        sb2_loaded = sem("sb2_loaded")
        rbias_loaded = sem("rbias_loaded")
        resid_loaded = sem("resid_loaded")
        pool_chain = sem("pool_chain")
        consts_ready = sem("consts_ready")
        dve_chain = sem("dve_chain")
        embed_done = sem("embed_done")
        hi_ready = sem("hi_ready")
        lo_ready = sem("lo_ready")
        pool_lo_ready = sem("pool_lo_ready")
        half_done = sem("half_done")
        hT_ready = sem("hT_ready")
        q_ready = sem("q_ready")
        sel_qk_ready = sem("sel_qk_ready")
        scores_done = sem("scores_done")
        sig_done = sem("sig_done")
        q1_ready = sem("q1_ready")
        hT_cleared = sem("hT_cleared")
        att_cleared = sem("att_cleared")
        tr_done = sem("tr_done")
        vt_cleared = sem("vt_cleared")
        v_ready = sem("v_ready")
        av_done = sem("av_done")
        zT_ready = sem("zT_ready")
        ztr_done = sem("ztr_done")
        stats_ready = sem("stats_ready")
        mv_ready = sem("mv_ready")
        vareps_ready = sem("vareps_ready")
        rstd_ready = sem("rstd_ready")
        h1_ready = sem("h1_ready")
        h1_stored = sem("h1_stored")
        h1tr_done = sem("h1tr_done")
        h1T_ready = sem("h1T_ready")
        logits_done = sem("logits_done")
        shifted_ready = sem("shifted_ready")
        exp_done = sem("exp_done")
        sel_ready = sem("sel_ready")
        prefix_done = sem("prefix_done")
        in_tile_ready = sem("in_tile_ready")
        ids_ready = sem("ids_ready")
        at_pos_ready = sem("at_pos_ready")
        rw_ready = sem("rw_ready")
        diag_ready = sem("diag_ready")
        index_done = sem("index_done")
        eid_ready = sem("eid_ready")
        spare_ready = sem("spare_ready")
        idx_ready = sem("idx_ready")
        dest_ready = sem("dest_ready")
        xg_loaded = [sem(f"xg_loaded{i}") for i in range(2)]
        xtr_done = sem("xtr_done")
        xT_ready = sem("xT_ready")
        mm1_done = sem("mm1_done")
        sup_done = sem("sup_done")
        sup1_ready = sem("sup1_ready")
        sgated_ready = sem("sgated_ready")
        shid_ready = sem("shid_ready")
        up1_ready = sem("up1_ready")
        up3_ready = sem("up3_ready")
        gated_ready = sem("gated_ready")
        hid_ready = sem("hid_ready")
        htr_done = sem("htr_done")
        hidT_ready = sem("hidT_ready")
        mm2_done = sem("mm2_done")
        y_ready = sem("y_ready")
        resid_ready = sem("resid_ready")
        y_stored = [sem(f"y_stored{i}") for i in range(2)]
        yg_loaded = [sem(f"yg_loaded{i}") for i in range(NT)]
        mix0_ready = sem("mix0_ready")
        mix_ready = sem("mix_ready")
        sum_done = sem("sum_done")
        stats2_ready = sem("stats2_ready")
        mv2_ready = sem("mv2_ready")
        vareps2_ready = sem("vareps2_ready")
        rstd2_ready = sem("rstd2_ready")
        nmr2_ready = sem("nmr2_ready")
        final_ready = [sem(f"final_ready{i}") for i in range(len(BATCHES))]
        out_stored = sem("out_stored")

        SF = 2 * GRP
        UNITS = NT // GRP * NHC
        UF = UNITS - 2

        def shared_place(t):
            return t if t < SF else t + R

        LOOP0 = 4
        LOOP1 = R - 1

        def split_count(n, i):
            return 2 * (i + 1) if n == 0 else 2 * len(SLICES) + 2 * (n - 1) + i + 1

        def ln_bank(u):
            return ps_hi[:, (1, 3)[u], :]

        def query_operands(t, u, c):
            shape = [P, HPC, TI, IMG]
            return (qx[u][:, c, :, :].rearrange("p h (i q) -> p h i q", i=TI),
                    hT_images[:, c, bass.ds(t * TI, TI), 0:IMG].unsqueeze(1).broadcast_to(shape),
                    sel_qk[:, c, :].unsqueeze(2).unsqueeze(3).broadcast_to(shape))

        POOL_FROM = 2

        def bank_pair(i):
            return (i + 1) % 2 if i < UF else (i - UF + 1) % 2

        def y_bank(t):
            return ps_hi[:, 0 if t % 2 == 1 and t != SF - 1 else 3, 0:D]

        def routed_y_bank(r):
            return ps_hi[:, 0 if isinstance(r, int) and r == R - 1 else 3, 0:D]

        def sum_of(t):
            if t < DT:
                return acc[:, t, :]
            banks = [ps_hi[:, 2]] + [ps_lo[:, i] for i in (2, 3, 0, 1)] + [ps_hi[:, 1]]
            return banks[t - DT][:, 0:D]

        def small_inputs():
            return [(bias_d[:, :], tok_b), (qk[:, 0, :], bq), (qk[:, 1, :], bk),
                    (vrow[:, :], bv_row.partition_broadcast(P)),
                    (gwT[:, :, :], gate_wT.rearrange("(c p) e -> p c e", p=P)),
                    (gb[:, :], gate_b.partition_broadcast(P))]

        block = ctx.enter_context(nc.Block())

        @block.sync
        def _(sp):
            s, m = CHUNKS[0]
            for i, (a, b) in enumerate(SLICES):
                sp.dma_start(wT[:, a:b, :],
                             tok_wT[a * P:b * P, :].rearrange("(k p) d -> p k d", p=P)).then_inc(slice_loaded[i], 16)
                sp.dma_start(patch[:, a:b, s:s + m], patches_T[a * P:b * P, s:s + m].rearrange(
                    "(k p) t -> p k t", p=P)).then_inc(slice_loaded[i], 16)
            for n, (s, m) in list(enumerate(CHUNKS))[1:]:
                sp.dma_start(patch[:, :, s:s + m],
                             patches_T[:, s:s + m].rearrange("(k p) t -> p k t", p=P)).then_inc(patch_loaded[n], 16)
                if n == 1:
                    for dst, src in small_inputs():
                        sp.dma_start(dst, src).then_inc(small_loaded, 16)
            full_rows = (HID // P) * P
            sp.dma_start(sb13[:, :, :], sb13_T).then_inc(sbias_loaded, 16)
            for e, (a, c, d) in [(SH, (sw1, sw3, sw2))] + [(e, (w1[e], w3[e], w2[e])) for e in range(E)]:
                for i, w in enumerate((a, c)):
                    sp.dma_start(w13[:, :, e * H2 + i * HID:e * H2 + (i + 1) * HID],
                                 w.rearrange("(c p) n -> p c n", p=P)).then_inc(weights_loaded, 16)
                sp.dma_start(w2s[:, 0:HID // P, e * D:(e + 1) * D],
                             d[0:full_rows, :].rearrange("(c p) n -> p c n", p=P)).then_inc(weights_loaded, 16)
                sp.dma_start(w2s[0:HID - full_rows, NHC - 1, e * D:(e + 1) * D],
                             d[full_rows:HID, :]).then_inc(weights_loaded, 16)
            with sp.Fori(0, NA - 1) as t:
                sp.wait_ge(h1_ready, t + 1)
                sp.dma_start(h1_dram[bass.ds(t * TT, TT), :], htok[0:TT, bass.ds(t, 1), :]).then_inc(h1_stored, 16)
            sp.wait_ge(h1_ready, NA)
            sp.dma_start(h1_dram[(NA - 1) * TT:TOK, :], htok[0:TT, NA - 1, :]).then_inc(h1_stored, 16)
            sp.wait_ge(av_done, NA)
            sp.dma_start(b2b[:, SH * D:(SH + 1) * D], sb2.partition_broadcast(P)).then_inc(sb2_loaded, 16)
            sp.wait_ge(h1_stored, 16 * NA)
            sp.wait_ge(h1tr_done, NA)
            sp.dma_start(resid[:, 0:NT, :], h1_dram.rearrange("(t p) d -> p t d", p=P)).then_inc(resid_loaded, 16)
            for i, b in enumerate((b1, b3)):
                sp.dma_start(b13[:, 0:E * H2].rearrange("p (e x) -> p e x", e=E)[:, :, i * HID:(i + 1) * HID],
                             b.partition_broadcast(P)).then_inc(rbias_loaded, 16)
            sp.dma_start(b2b[:, 0:E * D].rearrange("p (e x) -> p e x", e=E),
                         b2.partition_broadcast(P)).then_inc(rbias_loaded, 16)

            sp.wait_ge(y_stored[0], 16 * ((R + 1) // 2))
            sp.wait_ge(y_stored[1], 16 * (R // 2))
            for t in range(NT):
                sp.dma_start(yg[:, t, :, :], y_dram[TOP * t * P:TOP * (t + 1) * P, :].rearrange(
                    "(p k) d -> p k d", k=TOP)).then_inc(yg_loaded[t], 16)
            for i, (a, b) in enumerate(BATCHES):
                sp.wait_ge(final_ready[i], b - a)
                sp.dma_start(out[a * P:b * P, :].rearrange("(t p) d -> p t d", p=P),
                             acc[:, a:b, :]).then_inc(out_stored, 16)
            sp.wait_ge(out_stored, 16 * len(BATCHES))

        @block.gpsimd
        def _(pool):
            chain = [0]

            def link(ins):
                chain[0] += 1
                ins.then_inc(pool_chain, 1)
                pool.wait_ge(pool_chain, chain[0])

            nc.gpsimd.memset(half_neg[:, :], -0.5)
            nc.gpsimd.memset(eps[:, :], EPS)
            nc.gpsimd.memset(neg_one[:, :], -1.0)
            nc.gpsimd.iota(part[:, :], [[0, 1]], base=0, channel_multiplier=1)
            nc.gpsimd.iota(iota_row[:, :], [[1, P]], base=0, channel_multiplier=0)
            nc.gpsimd.memset(zeros[:, :], 0.0)
            link(nc.gpsimd.memset(ones_f[:, :], 1.0))
            nc.gpsimd.affine_select(out=ident[:, :], in_=ones_f[:, :], compare_op=ALU.is_equal, fill=0.0, base=0,
                                    pattern=[[-1, P]], channel_multiplier=1)
            nc.gpsimd.affine_select(out=before[:, :], in_=ones_f[:, :], compare_op=ALU.is_gt, fill=0.0, base=0,
                                    pattern=[[1, P]], channel_multiplier=-1)
            nc.gpsimd.affine_select(out=tri_i[:, :, :], in_=ones_f[:, 0:E * E].rearrange("p (e j) -> p e j", e=E),
                                    compare_op=ALU.is_gt, fill=0.0, base=0,
                                    pattern=[[1, E], [-1, E]], channel_multiplier=0)
            link(nc.gpsimd.affine_select(out=mask_bf[:, :], in_=zeros[:, :], compare_op=ALU.is_ge, fill=MASKED,
                                         base=0, pattern=[[1, IMG]], channel_multiplier=-1))
            nc.gpsimd.tensor_copy(ident_bf[:, :], ident[:, :])
            nc.gpsimd.tensor_copy(ones_bf[:, :], ones_f[:, :])
            nc.gpsimd.tensor_copy(iota_f[:, :], iota_row[:, :])
            nc.gpsimd.tensor_copy(iota_b[:, :], iota_row[:, :])
            link(nc.gpsimd.tensor_copy(part_f[:, :], part[:, :]))
            nc.gpsimd.memset(sel[:, NT, :], 0.0).then_inc(consts_ready, 1)

            def inverse_deviation(t, u, rows):
                pool.wait_ge(mv_ready, t + 1)
                nc.gpsimd.tensor_tensor(var_eps[0:rows, u, :], mv[0:rows, u, 1:2], eps[0:rows, :],
                                        ALU.add).then_inc(vareps_ready, 1)
                pool.wait_ge(vareps_ready, t + 1)
                nc.gpsimd.tensor_tensor(rstd[0:rows, u, :], var_eps[0:rows, u, :], half_neg[0:rows, :],
                                        ALU.pow).then_inc(rstd_ready, 1)

            nc.gpsimd.iota(idx[:, :], [[P, R]], base=TOP * TOK, channel_multiplier=1).then_inc(pool_chain, 1)
            pool.wait_ge(pool_chain, chain[0] + 1)
            nc.gpsimd.tensor_copy(spare[:, :], idx[:, :]).then_inc(spare_ready, 1)
            nc.gpsimd.memset(hT_images[:, :, :, IMG:PL], 0.0).then_inc(hT_cleared, 1)
            for i in range(2):
                nc.gpsimd.memset(vt[i][:, :], 0.0).then_inc(vt_cleared, 1)
                nc.gpsimd.memset(att[i][:, :, :], 0.0).then_inc(att_cleared, 1)

            def second_queries(t, u):
                pool.wait_ge(sel_qk_ready, 1)
                pool.wait_ge(hT_ready, C if isinstance(t, int) and t < 2 else C * len(CHUNKS))
                if not isinstance(t, int) or t >= 2:
                    pool.wait_ge(scores_done, t * C - C)
                nc.gpsimd.tensor_tensor(*query_operands(t, u, 1), ALU.mult).then_inc(q1_ready, 1)

            second_queries(0, 0)
            a, b = HALVES[1]
            for n, (s, m) in list(enumerate(CHUNKS))[POOL_FROM:]:
                pool.wait_ge(patch_loaded[n], 16)
                pool.wait_ge(hi_ready, split_count(n, 1))
                pool.wait_ge(embed_done, C * (n - 1))
                nc.gpsimd.tensor_tensor(patch_lo[n % 2][:, a:b, 0:m], patch[:, a:b, s:s + m],
                                        patch_hi[n % 2][:, a:b, 0:m], ALU.subtract).then_inc(pool_lo_ready, 1)
                second_queries(n - 1, n - 1 & 1)
            with pool.Fori(1, NA - 4, 2) as t:
                second_queries(t + 2, 1)
                inverse_deviation(t - 1, 0, TT)
                second_queries(t + 3, 0)
                inverse_deviation(t, 1, TT)
            second_queries(NA - 1, 1)
            for t in range(NA - 4, NA):
                inverse_deviation(t, t % 2, TT)

            pool.wait_ge(sb2_loaded, 16)
            pool.wait_ge(resid_loaded, 16)
            for g in range(NT // GRP):
                r = resid[:, g * GRP:(g + 1) * GRP, :]
                nc.gpsimd.tensor_tensor(r, r, b2b[:, SH * D:(SH + 1) * D].unsqueeze(1).broadcast_to([P, GRP, D]),
                                        ALU.add).then_inc(resid_ready, 1)

            def gather(r):
                if r >= 2:
                    pool.wait_ge(xg_loaded[r % 2], 16 * (r // 2))
                    pool.wait_ge(xtr_done, r - 1)
                nc.gpsimd.indirect_dma_start(
                    out=xg[:, r % 2, :], out_offset=None, in_=h1_dram,
                    in_offset=bass.IndirectOffsetOnAxis(ap=idx[:, r:r + 1], axis=0),
                ).then_inc(xg_loaded[r % 2], 16)

            def scatter(r):
                pool.wait_ge(y_ready, SF + r + 1)
                nc.gpsimd.indirect_dma_start(
                    out=y_dram, out_offset=bass.IndirectOffsetOnAxis(ap=dest[:, r:r + 1], axis=0),
                    in_=yb[:, r % 2, :], in_offset=None,
                ).then_inc(y_stored[r % 2], 16)

            nc.gpsimd.memset(ids[:, 0:NT, 2 * R:3 * R], 0.0)
            pool.wait_ge(in_tile_ready, 1)
            nc.gpsimd.tensor_tensor(ids[:, :, 0:R], in_tile,
                                    part_f[:, :].unsqueeze(1).broadcast_to([P, TOP * NT, R]), ALU.mult)
            for k in range(TOP):
                nc.gpsimd.tensor_tensor(ids[:, k * NT:(k + 1) * NT, R:2 * R], in_tile[:, k * NT:(k + 1) * NT, :],
                                        iota_f[:, 0:NT].unsqueeze(2).broadcast_to([P, NT, R]), ALU.mult)
            nc.gpsimd.tensor_copy(ids[:, NT:2 * NT, 2 * R:3 * R], in_tile[:, NT:2 * NT, :]).then_inc(ids_ready, 1)
            pool.wait_ge(h1_stored, 16 * NA)
            pool.wait_ge(idx_ready, 1)
            LAG = 5
            for r in range(R + LAG):
                if r < R:
                    gather(r)
                if r == LAG:
                    pool.wait_ge(dest_ready, 1)
                if r >= LAG:
                    scatter(r - LAG)
            for i, (a, b) in enumerate(BATCHES):
                pool.wait_ge(mv2_ready, b)
                nc.gpsimd.tensor_tensor(var_eps2[:, a:b], mv2[:, a:b, 1], eps[:, :].broadcast_to([P, b - a]),
                                        ALU.add).then_inc(vareps2_ready, 1)
                pool.wait_ge(vareps2_ready, i + 1)
                nc.gpsimd.tensor_tensor(rstd2[:, a:b], var_eps2[:, a:b], half_neg[:, :].broadcast_to([P, b - a]),
                                        ALU.pow).then_inc(rstd2_ready, 1)
                pool.wait_ge(rstd2_ready, i + 1)
                nc.gpsimd.tensor_tensor(nmr2[:, a:b], mv2[:, a:b, 0], rstd2[:, a:b],
                                        ALU.mult).then_inc(nmr2_ready, 1)
                pool.wait_ge(nmr2_ready, 2 * i + 1)
                nc.gpsimd.tensor_tensor(nmr2[:, a:b], nmr2[:, a:b], neg_one[:, :].broadcast_to([P, b - a]),
                                        ALU.mult).then_inc(nmr2_ready, 1)

        @block.scalar
        def _(act):
            def keep_hT(n):
                s, m = CHUNKS[n]
                for c in range(C):
                    act.wait_ge(embed_done, C * n + c + 1)
                    nc.scalar.activation(hT_images[:, c, s // IMG:(s + m) // IMG, 0:IMG],
                                         ps_hi[:, (n % 2) * C + c, 0:m].rearrange("p (i q) -> p i q", q=IMG),
                                         ACT.Identity,
                                         bias=bias_d[:, c:c + 1]).then_inc(hT_ready, 1)

            def sigmoid(t, u, rows):
                if not isinstance(t, int) or t >= 2:
                    act.wait_ge(av_done, t - 1)
                act.wait_ge(scores_done, t * C + C)
                for i in range(TI):
                    keys, queries = slice(i * PL, i * PL + IMG), slice(i * IMG, (i + 1) * IMG)
                    nc.scalar.activation(
                        att[u][keys, :, queries].rearrange("p (c h) q -> p c h q", c=C),
                        ps_lo[keys, C * u:C * (u + 1), 0:HPC * IMG].rearrange("p c (h q) -> p c h q", h=HPC),
                        ACT.Sigmoid).then_inc(sig_done, 1)

            def keep_h1T(t, u, rows=TT):
                act.wait_ge(h1tr_done, t + 1)
                nc.scalar.activation(h1T[:, :, bass.ds(t * TT, rows)],
                                     ln_bank(u)[:, 0:C * rows].rearrange("p (c t) -> p c t", c=C),
                                     ACT.Copy).then_inc(h1T_ready, 1)

            for i, (a, b) in enumerate(SLICES):
                act.wait_ge(slice_loaded[i], 32)
                nc.scalar.activation(w_hi[:, a:b, :], wT[:, a:b, :], ACT.Copy).then_inc(hi_ready, 1)
                nc.scalar.activation(patch_hi[0][:, a:b, 0:CH], patch[:, a:b, 0:CH],
                                     ACT.Copy).then_inc(hi_ready, 1)
            for n, (s, m) in list(enumerate(CHUNKS))[1:]:
                act.wait_ge(patch_loaded[n], 16)
                for i, (a, b) in enumerate(HALVES):
                    if n >= 2:
                        act.wait_ge(*((half_done, n - 1) if i == 0 else (embed_done, C * (n - 1))))
                    nc.scalar.activation(patch_hi[n % 2][:, a:b, 0:m], patch[:, a:b, s:s + m],
                                         ACT.Copy).then_inc(hi_ready, 1)
                if n == 1:
                    act.wait_ge(small_loaded, 16 * len(small_inputs()))
                    act.wait_ge(hT_cleared, 1)
                keep_hT(n - 1)
            act.wait_ge(att_cleared, 2)
            sigmoid(0, 0, TT)
            keep_hT(len(CHUNKS) - 1)
            sigmoid(1, 1, TT)
            sigmoid(2, 0, TT)
            with act.Fori(2, NA - 3, 2) as t:
                sigmoid(t + 1, 1, TT)
                keep_h1T(t - 2, 0)
                sigmoid(t + 2, 0, TT)
                keep_h1T(t - 1, 1)
            sigmoid(NA - 1, 1, TT)
            keep_h1T(NA - 4, 0)
            keep_h1T(NA - 3, 1)

            def shared_up1(i):
                rows, u, m = HC[i % NHC][1], bank_pair(i), i % NHC
                act.wait_ge(sup_done, i + 1)
                if i >= 2:
                    act.wait_ge(sgated_ready, i - 1)
                if i == UF:
                    act.wait_ge(gated_ready, R)
                    act.wait_ge(hid_ready, R)
                nc.scalar.activation(sup1[0:rows, u, :], ps_lo[0:rows, 2 * u, 0:GT], ACT.Identity,
                                     bias=sb13[0:rows, 0, m:m + 1]).then_inc(sup1_ready, 1)

            def shared_silu(i):
                rows, u, g, m = HC[i % NHC][1], bank_pair(i), i // NHC, i % NHC
                act.wait_ge(sgated_ready, i + 1)
                if i == 2 * NHC:
                    act.wait_ge(mm2_done, GRP)
                nc.scalar.activation(hsT[0:rows, g % 2, m, :], sgated[0:rows, u, :],
                                     ACT.Silu).then_inc(shid_ready, 1)

            act.wait_ge(sbias_loaded, 16)
            shared_up1(0)
            keep_h1T(NA - 2, 0)
            shared_up1(1)
            keep_h1T(NA - 1, 1)
            act.wait_ge(shifted_ready, 1)
            nc.scalar.activation(lex[:, :, :], lg[:, :, :], ACT.Exp).then_inc(exp_done, 1)
            shared_silu(0)
            shared_silu(1)
            for i in range(2, UF):
                shared_up1(i)
                shared_silu(i)

            def keep_xT(r, u):
                act.wait_ge(xtr_done, r + 1)
                if not isinstance(r, int) or r >= 2:
                    act.wait_ge(mm1_done, r - 1)
                nc.scalar.activation(xT[:, u, :], ps_hi[:, 0, 0:C * P], ACT.Copy).then_inc(xT_ready, 1)

            def silu(r, u):
                act.wait_ge(gated_ready, r + 1)
                if not isinstance(r, int) or r >= 2:
                    act.wait_ge(htr_done, r - 1)
                nc.scalar.activation(hid[:, u, :], gated[:, u, :], ACT.Silu).then_inc(hid_ready, 1)

            def keep_hidT(r, u):
                act.wait_ge(htr_done, r + 1)
                if not isinstance(r, int) or r >= 2:
                    act.wait_ge(mm2_done, SF + r - 1)
                nc.scalar.activation(hidT[:, u, 0:NHC - 1, :], ps_hi[:, 1, 0:(NHC - 1) * P], ACT.Copy)
                rows = HC[-1][1]
                nc.scalar.activation(hidT[0:rows, u, NHC - 1, :], ps_hi[0:rows, 1, (NHC - 1) * P:NHC * P],
                                     ACT.Copy).then_inc(hidT_ready, 1)

            def step(r, u):
                if not isinstance(r, int) or r + 1 < R:
                    keep_xT(r + 1, 1 - u)
                if not isinstance(r, int) or r >= 1:
                    keep_hidT(r - 1, 1 - u)
                silu(r, u)

            def diagonals(t):
                act.wait_ge(rw_ready, 1)
                for k in range(TOP):
                    nc.scalar.activation(diag[:, t - DT, k, :], ident[:, :], ACT.Copy,
                                         scale=rw[:, k, t:t + 1]).then_inc(diag_ready, 1)

            keep_xT(0, 0)
            for r in range(LOOP0):
                step(r, r % 2)
                diagonals(DT + r)
            for t in range(DT + LOOP0, NT):
                diagonals(t)
            with act.Fori(LOOP0, LOOP1 - 1, 2) as r:
                step(r, 0)
                step(r + 1, 1)
            for r in range(LOOP1, R):
                step(r, r % 2)
            shared_up1(UF)
            keep_hidT(R - 1, (R - 1) % 2)
            shared_silu(UF)
            shared_up1(UF + 1)
            shared_silu(UF + 1)
            for i, (a, b) in enumerate(BATCHES):
                act.wait_ge(nmr2_ready, 2 * (i + 1))
                for t in range(a, min(b, NT - 2)):
                    nc.scalar.activation(acc[:, t, :], sum_of(t), ACT.Identity, scale=rstd2[:, t:t + 1],
                                         bias=nmr2[:, t:t + 1]).then_inc(final_ready[i], 1)

        @block.vector
        def _(dve):
            chain = [0]

            def link(ins):
                chain[0] += 1
                ins.then_inc(dve_chain, 1)
                dve.wait_ge(dve_chain, chain[0])

            v = nc.vector

            def keep_rest(rest, x, hi, done):
                dve.wait_ge(hi_ready, done)
                v.tensor_tensor(rest, x, hi, ALU.subtract).then_inc(lo_ready, 1)

            def rest_of_chunk(n):
                s, m = CHUNKS[n]
                dve.wait_ge(patch_loaded[n], 16)
                for i, (a, b) in enumerate(HALVES if n < POOL_FROM else HALVES[:1]):
                    if n >= 2:
                        dve.wait_ge(half_done, n - 1)
                    keep_rest(patch_lo[n % 2][:, a:b, 0:m], patch[:, a:b, s:s + m], patch_hi[n % 2][:, a:b, 0:m],
                              split_count(n, i))

            for i, (a, b) in enumerate(SLICES):
                dve.wait_ge(slice_loaded[i], 32)
                keep_rest(w_lo[:, a:b, :], wT[:, a:b, :], w_hi[:, a:b, :], 2 * i + 1)
                keep_rest(patch_lo[0][:, a:b, 0:CH], patch[:, a:b, 0:CH], patch_hi[0][:, a:b, 0:CH], 2 * i + 2)
            rest_of_chunk(1)
            dve.wait_ge(consts_ready, 1)
            link(v.tensor_scalar(head_i[:, :], part[:, :], 4, None, ALU.arith_shift_right))
            link(v.tensor_copy(head_f[:, :], head_i[:, :]))
            v.tensor_scalar(own_head[:, :], iota_f[:, 0:HPC], head_f[:, :], None, ALU.is_equal)
            v.tensor_scalar(full[:, :], iota_f[:, 0:NT], float(P), None, ALU.mult)
            dve.wait_ge(small_loaded, 16 * len(small_inputs()))
            for i in range(2):
                v.tensor_scalar(sgn[:, i, :], qk[:, i, :], 0.0, None, ALU.is_gt)
                v.tensor_scalar(sgn[:, 2 + i, :], qk[:, i, :], 0.0, None, ALU.is_lt)
            v.tensor_scalar(vs[:, 0, :], vrow[:, :], 0.0, None, ALU.is_gt)
            link(v.tensor_scalar(vs[:, 1, :], vrow[:, :], 0.0, None, ALU.is_lt))
            link(v.tensor_tensor(sgn[:, 4:6, :], sgn[:, 0:2, :], sgn[:, 2:4, :], ALU.subtract))
            link(v.tensor_tensor(sgn_v[:, :], vs[:, 0, :], vs[:, 1, :], ALU.subtract))
            link(v.tensor_tensor(sgn_qk[:, :], sgn[:, 4, :], sgn[:, 5, :], ALU.mult))
            for c in range(C):
                last = v.tensor_scalar(sel_qk[:, c, :], own_head[:, :], sgn_qk[:, c:c + 1], None, ALU.mult)
            last.then_inc(sel_qk_ready, 1)
            dve.wait_ge(sel_qk_ready, 1)

            def queries(t, u):
                if not isinstance(t, int) or t >= 2:
                    dve.wait_ge(scores_done, t * C - C - 1)
                v.tensor_tensor(*query_operands(t, u, 0), ALU.mult).then_inc(q_ready, 1)

            def values(t, u, rows):
                if isinstance(t, int) and t == 0:
                    dve.wait_ge(vt_cleared, 2)
                dve.wait_ge(tr_done, t + 1)
                if not isinstance(t, int) or t >= 2:
                    dve.wait_ge(av_done, t - 1)
                heads = vt[u][0:rows, :].rearrange("p (h x) -> p h x", x=64)
                for j in range(2):
                    last = v.tensor_tensor(heads[:, :, 48 * j:48 * j + HD],
                                           ps_hi[0:rows, 2, 0:D].rearrange("p (h j x) -> p h j x", j=2, x=HD)[:, :, j, :],
                                           sgn_v[0:rows, :].rearrange("p (h j x) -> p h j x", j=2, x=HD)[:, :, j, :],
                                           ALU.mult)
                last.then_inc(v_ready, 1)

            def residual(t, u, rows):
                dve.wait_ge(av_done, t + 1)
                if not isinstance(t, int) or t >= 2:
                    dve.wait_ge(ztr_done, t - 1)
                v.tensor_tensor(zT[:, u, :].rearrange("p (c i q) -> p c i q", c=C, i=TI),
                                ps_hi[:, 0, 0:C * TT].rearrange("p (c i q) -> p c i q", c=C, i=TI),
                                hT_images[:, :, bass.ds(t * TI, TI), 0:IMG], ALU.add).then_inc(zT_ready, 1)

            def statistics(t, u):
                dve.wait_ge(ztr_done, t + 1)
                v.bn_stats(stats[0:TT, u, :], ln_bank(u)[0:TT, 0:D]).then_inc(stats_ready, 1)

            def moments(t, u):
                dve.wait_ge(consts_ready, 1)
                dve.wait_ge(stats_ready, t + 1)
                v.bn_aggr(mv[0:TT, u, :], stats[0:TT, u, :]).then_inc(mv_ready, 1)

            def normalise(t, u):
                dve.wait_ge(rstd_ready, t + 1)
                v.tensor_scalar(htok[0:TT, bass.ds(t, 1), :], ln_bank(u)[0:TT, 0:D],
                                mv[0:TT, u, 0:1], rstd[0:TT, u, :], ALU.subtract,
                                ALU.mult).then_inc(h1_ready, 1)

            def tile(t, u, ahead=2):
                if ahead == 2:
                    queries(t + 2, u)
                if not isinstance(t, int) or t >= 2:
                    normalise(t - 2, u)
                if not isinstance(t, int) or t >= 1:
                    statistics(t - 1, 1 - u)
                residual(t, u, TT)
                if not isinstance(t, int) or t >= 1:
                    moments(t - 1, 1 - u)
                if ahead:
                    values(t + 1, 1 - u, P)

            rest_of_chunk(2)
            dve.wait_ge(hT_ready, C)
            queries(0, 0)
            rest_of_chunk(3)
            queries(1, 1)
            dve.wait_ge(hT_ready, C * len(CHUNKS))
            values(0, 0, P)
            tile(0, 0)
            tile(1, 1)
            with dve.Fori(2, NA - 3, 2) as t:
                tile(t, 0)
                tile(t + 1, 1)
            tile(NA - 2, 0, 1)
            tile(NA - 1, 1, 0)
            normalise(NA - 2, 0)
            statistics(NA - 1, 1)
            moments(NA - 1, 1)

            def softmax():
                dve.wait_ge(logits_done, 1)
                lgp = ps_hi[:, 2, D:D + NT * E].rearrange("p (t e) -> p t e", e=E)
                link(v.tensor_reduce(lmax[:, :], lgp, AX.X, ALU.max))
                v.tensor_tensor(lg[:, :, :], lgp, lmax[:, :].unsqueeze(2).broadcast_to([P, NT, E]),
                                ALU.subtract).then_inc(shifted_ready, 1)
                dve.wait_ge(exp_done, 1)
                link(v.tensor_reduce(lsum[:, :], lex[:, :, :], AX.X, ALU.add))
                link(v.reciprocal(lrec[:, :], lsum[:, :]))
                link(v.tensor_tensor(probs[:, :, :], lex[:, :, :], lrec[:, :].unsqueeze(2).broadcast_to([P, NT, E]),
                                     ALU.mult))
                link(v.tensor_tensor(biased[:, :, :], probs[:, :, :], gb[:, :].unsqueeze(1).broadcast_to([P, NT, E]),
                                     ALU.add))

            def compare():
                other = biased[:, :, :].unsqueeze(2).broadcast_to([P, NT, E, E])
                own = biased[:, :, :].unsqueeze(3).broadcast_to([P, NT, E, E])
                v.tensor_tensor(pair_a[:, :, :, :], other, own, ALU.is_gt)
                link(v.tensor_tensor(pair_b[:, :, :, :], other, own, ALU.is_equal))

            def select():
                link(v.tensor_tensor(pair_b[:, :, :, :], pair_b[:, :, :, :],
                                     tri_i[:, :, :].unsqueeze(1).broadcast_to([P, NT, E, E]), ALU.mult))
                link(v.tensor_tensor(pair_a[:, :, :, :], pair_a[:, :, :, :], pair_b[:, :, :, :], ALU.add))
                link(v.tensor_reduce(rank[:, :, :], pair_a[:, :, :, :], AX.X, ALU.add))
                v.tensor_scalar(sel[:, 0:NT, :], rank[:, :, :], float(TOP), None, ALU.is_lt).then_inc(sel_ready, 1)
                for k in range(TOP):
                    last = v.tensor_scalar(hot[:, k, :, :], rank[:, :, :], float(k), None, ALU.is_equal)
                link(last)
                link(v.tensor_tensor(tmp[:, :, :, :], hot[:, :, :, :],
                                     probs[:, :, :].unsqueeze(1).broadcast_to([P, TOP, NT, E]), ALU.mult))
                v.tensor_reduce(rw[:, :, :], tmp[:, :, :, :], AX.X, ALU.add).then_inc(rw_ready, 1)

            def gate(r, u):
                e = dve.value_load(eid[0:1, bass.ds(r, 1)], min_val=0, max_val=E - 1)
                dve.wait_ge(mm1_done, r + 1)
                if not isinstance(r, int) or r >= 1:
                    dve.wait_ge(gated_ready, r)
                for i, (dst, done) in enumerate(((up1, up1_ready), (up3, up3_ready))):
                    v.tensor_tensor(dst, ps_lo[:, u * 2 + i, 0:HID], b13[:, bass.ds(e * H2 + i * HID, HID)],
                                    ALU.add).then_inc(done, 1)
                dve.wait_ge(up1_ready, r + 1)
                dve.wait_ge(up3_ready, r + 1)
                if isinstance(r, int) and r == 0:
                    dve.wait_ge(shid_ready, UF)
                if not isinstance(r, int) or r >= 2:
                    dve.wait_ge(hid_ready, r - 1)
                v.tensor_tensor(gated[:, u, :], up1, up3, ALU.mult).then_inc(gated_ready, 1)

            def keep_y(r, u):
                dve.wait_ge(mm2_done, SF + r + 1)
                e = dve.value_load(eid[0:1, bass.ds(r, 1)], min_val=0, max_val=E - 1)
                if not isinstance(r, int) or r >= 2:
                    dve.wait_ge(y_stored[u], r // 2 * 16 if isinstance(r, int) else (r - u) * 8)
                v.tensor_tensor(yb[:, u, :], routed_y_bank(r), b2b[:, bass.ds(e * D, D)],
                                ALU.add).then_inc(y_ready, 1)

            def shared_gate(i):
                rows, u, m = HC[i % NHC][1], bank_pair(i), i % NHC
                dve.wait_ge(sup1_ready, i + 1)
                if i >= 2:
                    dve.wait_ge(shid_ready, i - 1)
                if i == UF:
                    dve.wait_ge(hid_ready, R)
                    dve.wait_ge(htr_done, R)
                v.scalar_tensor_tensor(out=sgated[0:rows, u, :], in0=ps_lo[0:rows, 2 * u + 1, 0:GT],
                                       scalar=sb13[0:rows, 1, m:m + 1], in1=sup1[0:rows, u, :],
                                       op0=ALU.add, op1=ALU.mult).then_inc(sgated_ready, 1)

            def keep_shared(t):
                dve.wait_ge(mm2_done, shared_place(t) + 1)
                dve.wait_ge(resid_ready, t // GRP + 1)
                v.tensor_tensor(acc[:, t, :], y_bank(t), resid[:, t, :], ALU.add).then_inc(y_ready, 1)

            def step(r, u):
                gate(r, u)
                if not isinstance(r, int) or r >= 2:
                    keep_y(r - 2, u)

            def find_slots():
                dve.wait_ge(prefix_done, 1)
                count = ps_hi[:, 2, NT * E:NT * E + E]
                link(v.tensor_tensor(cmp_n[:, :, :], count.unsqueeze(2).broadcast_to([P, E, NT]),
                                     full[:, :].unsqueeze(1).broadcast_to([P, E, NT]), ALU.is_gt))
                link(v.tensor_reduce(ntile[:, :], cmp_n[:, :, :], AX.X, ALU.add))
                link(v.tensor_tensor(cmp_c[:, :, :], ntile[:, :].unsqueeze(1).broadcast_to([P, E, E]),
                                     tri_i[:, :, :], ALU.mult))
                link(v.tensor_reduce(tstart[:, :], cmp_c[:, :, :], AX.X, ALU.add))
                link(v.tensor_scalar(sstart[:, :], tstart[:, :], float(P), None, ALU.mult))
                link(v.tensor_tensor(place[:, :, :], ps_hi[:, 2, 0:NT * E].rearrange("p (t e) -> p t e", e=E),
                                     sstart[:, :].unsqueeze(1).broadcast_to([P, NT, E]), ALU.add))
                dve.wait_ge(rw_ready, 1)
                link(v.tensor_tensor(tmp[:, :, :, :], hot[:, :, :, :],
                                     place[:, :, :].unsqueeze(1).broadcast_to([P, TOP, NT, E]), ALU.mult))
                link(v.tensor_reduce(slot_f[:, :, :], tmp[:, :, :, :], AX.X, ALU.add))
                link(v.tensor_copy(slot[:, :], slot_f[:, :, :].rearrange("p k t -> p (k t)")))
                v.tensor_scalar(slot_hi[:, :], slot[:, :], 7, None, ALU.arith_shift_right)
                link(v.tensor_scalar(slot_lo[:, :], slot[:, :], P - 1, None, ALU.bitwise_and))
                v.tensor_copy(hi_b[:, :], slot_hi[:, :])
                link(v.tensor_copy(lo_b[:, :], slot_lo[:, :]))
                v.tensor_tensor(in_tile, iota_b[:, 0:R].unsqueeze(1).broadcast_to([P, TOP * NT, R]),
                                hi_b[:, :].unsqueeze(2).broadcast_to([P, TOP * NT, R]),
                                ALU.is_equal).then_inc(in_tile_ready, 1)

            def find_experts():
                link(v.tensor_tensor(tend[:, :], tstart[:, :], ntile[:, :], ALU.add))
                link(v.tensor_tensor(cmp_e[:, :, :], iota_f[:, 0:R].unsqueeze(2).broadcast_to([P, R, E]),
                                     tend[:, :].unsqueeze(1).broadcast_to([P, R, E]), ALU.is_ge))
                link(v.tensor_reduce(eid_f[:, :], cmp_e[:, :, :], AX.X, ALU.add))
                link(v.tensor_scalar(eid_c[:, :], eid_f[:, :], float(E - 1), None, ALU.min))
                v.tensor_copy(eid[:, :], eid_c[:, :]).then_inc(eid_ready, 1)

            def positions(k):
                last = v.tensor_tensor(at_pos[:, k * NT:(k + 1) * NT, :],
                                       iota_b[:, :].unsqueeze(1).broadcast_to([P, NT, P]),
                                       lo_b[:, k * NT:(k + 1) * NT].unsqueeze(2).broadcast_to([P, NT, P]),
                                       ALU.is_equal)
                if k == TOP - 1:
                    last.then_inc(at_pos_ready, 1)

            def find_tokens():
                dve.wait_ge(index_done, 1)
                link(v.tensor_copy(idx_f[:, :], ps_hi[:, 2, 0:4 * R]))
                link(v.scalar_tensor_tensor(out=idx_f[:, 0:R], in0=idx_f[:, R:2 * R], scalar=float(P),
                                            in1=idx_f[:, 0:R], op0=ALU.mult, op1=ALU.add))
                dve.wait_ge(spare_ready, 1)
                v.tensor_copy(idx[:, :], idx_f[:, 0:R]).then_inc(idx_ready, 1)

            def find_rows():
                link(v.scalar_tensor_tensor(out=dest_f[:, :], in0=idx_f[:, 0:R], scalar=float(TOP),
                                            in1=idx_f[:, 2 * R:3 * R], op0=ALU.mult, op1=ALU.add))
                link(v.tensor_tensor(dest_f[:, :], dest_f[:, :], spare[:, :], ALU.subtract))
                link(v.tensor_tensor(dest_f[:, :], dest_f[:, :], idx_f[:, 3 * R:4 * R], ALU.mult))
                link(v.tensor_tensor(dest_f[:, :], dest_f[:, :], spare[:, :], ALU.add))
                v.tensor_copy(dest[:, :], dest_f[:, :]).then_inc(dest_ready, 1)

            dve.wait_ge(sbias_loaded, 16)
            shared_gate(0)
            normalise(NA - 1, 1)
            shared_gate(1)
            softmax()
            compare()
            shared_gate(2)
            select()
            shared_gate(3)
            find_slots()
            keep_shared(0)
            shared_gate(4)
            positions(0)
            keep_shared(1)
            positions(1)
            shared_gate(5)
            keep_shared(2)
            find_experts()
            find_tokens()
            for i in range(6, UF):
                shared_gate(i)
            keep_shared(3)
            find_rows()
            keep_shared(4)
            dve.wait_ge(eid_ready, 1)
            dve.wait_ge(rbias_loaded, 16 * 3)
            step(0, 0)
            keep_shared(5)
            for r in range(1, LOOP0):
                step(r, r % 2)
            with dve.Fori(LOOP0, LOOP1 - 1, 2) as r:
                step(r, 0)
                step(r + 1, 1)
            for r in range(LOOP1, R):
                step(r, r % 2)
            keep_y(R - 2, (R - 2) % 2)
            shared_gate(UF)
            keep_y(R - 1, (R - 1) % 2)
            shared_gate(UF + 1)
            for t in range(SF, NT - 1):
                keep_shared(t)

            def combine(t):
                dve.wait_ge(yg_loaded[t], 16)
                dve.wait_ge(y_ready, shared_place(t) + 1)
                for k, done in enumerate((mix0_ready, mix_ready)):
                    v.scalar_tensor_tensor(out=acc[:, t, :], in0=yg[:, t, k, :], scalar=rw[:, k, t:t + 1],
                                           in1=acc[:, t, :], op0=ALU.mult, op1=ALU.add).then_inc(done, 1)
                    dve.wait_ge(done, t + 1)

            def moments2(t):
                if t >= DT:
                    dve.wait_ge(sum_done, t - DT + 1)
                v.bn_stats(stats2[:, t, :], sum_of(t)).then_inc(stats2_ready, 1)
                dve.wait_ge(stats2_ready, t + 1)
                v.bn_aggr(mv2[:, t, :], stats2[:, t, :]).then_inc(mv2_ready, 1)

            def finish(i):
                dve.wait_ge(rstd2_ready, i + 1)
                for t in range(NT - 2, NT):
                    v.tensor_scalar(acc[:, t, :], sum_of(t), mv2[:, t, 0:1], rstd2[:, t:t + 1],
                                    ALU.subtract, ALU.mult).then_inc(final_ready[i], 1)

            for t in range(DT):
                combine(t)
                moments2(t)
                if t == 0:
                    keep_shared(NT - 1)
            for t in range(DT, NT):
                moments2(t)
            finish(len(BATCHES) - 1)

        @block.tensor
        def _(pe):
            mm = nc.tensor.matmul
            def embed(n):
                s, m = CHUNKS[n]
                if n >= 2:
                    pe.wait_ge(hT_ready, C * (n - 1))
                for i, (a, b) in enumerate(SLICES if n == 0 else HALVES):
                    pe.wait_ge(hi_ready, split_count(n, i))
                    if n >= POOL_FROM and i == 1:
                        pe.wait_ge(pool_lo_ready, n - POOL_FROM + 1)
                    else:
                        pe.wait_ge(lo_ready, split_count(n, i) - max(0, n - POOL_FROM))
                    for c in range(C):
                        for k in range(a, b):
                            ws = [w[:, k, c * P:(c + 1) * P] for w in (w_hi, w_lo)]
                            ps = [x[n % 2][:, k, 0:m] for x in (patch_hi, patch_lo)]
                            for j, (x, y) in enumerate(((1, 0), (0, 0), (0, 1))):
                                last = mm(ps_hi[:, (n % 2) * C + c, 0:m], ws[x], ps[y],
                                          start=(k == 0 and j == 0), stop=(k == KC - 1 and j == 2))
                        if b == KC:
                            last.then_inc(embed_done, 1)
                        elif b == KC // 2 and c == C - 1:
                            last.then_inc(half_done, 1)

            def scores(t, rows):
                if t >= 2:
                    pe.wait_ge(sig_done, TI * (t - 1))
                for c in range(C):
                    pe.wait_ge((q_ready, q1_ready)[c], t + 1)
                    banks = [ps_lo[i * PL:i * PL + IMG, C * (t % 2) + c, 0:HPC * IMG].rearrange(
                        "p (h q) -> p h q", h=HPC) for i in range(TI)]
                    for i in range(TI):
                        mm(banks[i], ident_bf[:, 0:IMG], mask_bf[:, :].unsqueeze(1).broadcast_to([P, HPC, IMG]),
                           start=True, stop=False)
                    for i in range(TI):
                        at = (t * TI + i) * PL
                        last = mm(banks[i], hT[:, c, at:at + IMG], qx[t % 2][:, c, :, i * IMG:(i + 1) * IMG],
                                  start=False, stop=True)
                    last.then_inc(scores_done, 1)

            def to_tokens(t, rows):
                if t >= 1:
                    pe.wait_ge(v_ready, t)
                for c in range(C):
                    last = nc.tensor.transpose(ps_hi[:, 2, c * P:(c + 1) * P], hT[:, c, t * P:(t + 1) * P],
                                               ident[:, :])
                last.then_inc(tr_done, 1)

            def attend(t, u, rows):
                pe.wait_ge(v_ready, t + 1)
                if t >= 1:
                    pe.wait_ge(zT_ready, t)
                pe.wait_ge(sig_done, TI * (t + 1))
                for c in range(C):
                    for j in range(2):
                        for g in range(GROUPS):
                            h = (c * GROUPS + g) * 2 + j
                            last = mm(ps_hi[32 * g:32 * g + 32, 0, c * rows:(c + 1) * rows],
                                      vt[u][:, h * 32:(h + 1) * 32], att[u][:, h, :],
                                      start=(j == 0), stop=(j == 1))
                last.then_inc(av_done, 1)

            def z_transpose(t, u, rows):
                pe.wait_ge(zT_ready, t + 1)
                if t >= 2:
                    pe.wait_ge(h1T_ready, t - 1)
                for c in range(C):
                    last = nc.tensor.transpose(ln_bank(u)[0:rows, c * P:(c + 1) * P],
                                               zT[:, u, c * rows:(c + 1) * rows], ident[:, :])
                last.then_inc(ztr_done, 1)

            def h1_transpose(t, rows):
                pe.wait_ge(h1_ready, t + 1)
                for c in range(C):
                    last = nc.tensor.transpose(ln_bank(t % 2)[:, c * rows:(c + 1) * rows],
                                               htok[0:rows, bass.ds(t, 1), c * P:(c + 1) * P], ident[0:rows, 0:rows])
                last.then_inc(h1tr_done, 1)

            def logits(t):
                pe.wait_ge(h1T_ready, t + 1)
                lo, hi = t * TT // P, (TOK if t == NA - 1 else (t + 1) * TT) // P
                for k in range(lo, hi):
                    for c in range(C):
                        last = mm(ps_hi[:, 2, D + k * E:D + (k + 1) * E], h1T[:, c, k * P:(k + 1) * P], gwT[:, c, :],
                                  start=(c == 0), stop=(c == C - 1))
                if t == NA - 1:
                    last.then_inc(logits_done, 1)

            def x_transpose(r, u):
                if isinstance(r, int) and r == 0:
                    pe.wait_ge(y_ready, SF - 2)
                pe.wait_ge(xg_loaded[u], 16 * (r // 2 + 1) if isinstance(r, int) else (r - u + 2) * 8)
                if not isinstance(r, int) or r >= 1:
                    pe.wait_ge(xT_ready, r)
                for c in range(C):
                    last = nc.tensor.transpose(ps_hi[:, 0, c * P:(c + 1) * P],
                                               xg[:, u, c * P:(c + 1) * P], ident[:, :])
                last.then_inc(xtr_done, 1)

            def up(r, u):
                e = pe.value_load(eid[0:1, bass.ds(r, 1)], min_val=0, max_val=E - 1)
                pe.wait_ge(xT_ready, r + 1)
                if isinstance(r, int) and r < 2:
                    pe.wait_ge(sgated_ready, UF)
                else:
                    pe.wait_ge(gated_ready, r - 1)
                for i in range(2):
                    for c in range(C):
                        last = mm(ps_lo[:, u * 2 + i, 0:HID], xT[:, u, c * P:(c + 1) * P],
                                  w13[:, c, bass.ds(e * H2 + i * HID, HID)], start=(c == 0), stop=(c == C - 1))
                last.then_inc(mm1_done, 1)

            def hid_transpose(r, u):
                pe.wait_ge(hid_ready, r + 1)
                if not isinstance(r, int) or r >= 1:
                    pe.wait_ge(hidT_ready, r)
                for j, (s, m) in enumerate(HC):
                    last = nc.tensor.transpose(ps_hi[0:m, 1, j * P:(j + 1) * P], hid[:, u, s:s + m], ident[:, :])
                last.then_inc(htr_done, 1)

            def down(r, u):
                e = pe.value_load(eid[0:1, bass.ds(r, 1)], min_val=0, max_val=E - 1)
                pe.wait_ge(hidT_ready, r + 1)
                if isinstance(r, int) and r == R - 1:
                    pe.wait_ge(xT_ready, R)
                else:
                    pe.wait_ge(y_ready, SF + r)
                for j, (s, m) in enumerate(HC):
                    last = mm(routed_y_bank(r), hidT[0:m, u, j, :], w2s[0:m, j, bass.ds(e * D, D)],
                              start=(j == 0), stop=(j == NHC - 1))
                last.then_inc(mm2_done, 1)

            def step(r, u):
                up(r, u)
                if not isinstance(r, int) or r + 1 < R:
                    x_transpose(r + 1, 1 - u)
                if not isinstance(r, int) or r >= 1:
                    hid_transpose(r - 1, 1 - u)
                if not isinstance(r, int) or r >= 2:
                    down(r - 2, u)

            def shared_up(i, halves=(0, 1)):
                g, m, u = i // NHC, i % NHC, bank_pair(i)
                s, rows = HC[m]
                if i < 2:
                    pe.wait_ge(sig_done, TI * NA)
                elif i < UF:
                    pe.wait_ge(sgated_ready, i - 1)
                else:
                    pe.wait_ge(gated_ready, R - 1 + i - UF)
                for j in halves:
                    at = SH * H2 + j * HID + s
                    for c in range(C):
                        last = mm(ps_lo[0:rows, 2 * u + j, 0:GT], w13[:, c, at:at + rows],
                                  h1T[:, c, g * GT:(g + 1) * GT], start=(c == 0), stop=(c == C - 1))
                    if j == 1:
                        last.then_inc(sup_done, 1)

            def shared_down(t):
                g, x = t // GRP, t % GRP * P
                pe.wait_ge(shid_ready, NHC * (g + 1))
                if t == 0:
                    pe.wait_ge(h1T_ready, NA)
                elif t == 1:
                    pe.wait_ge(zT_ready, NA)
                elif t < SF - 1:
                    pe.wait_ge(y_ready, t - 1)
                elif t == SF - 1:
                    pe.wait_ge(y_ready, t)
                elif t < SF + 2:
                    pe.wait_ge(y_ready, SF + R)
                else:
                    pe.wait_ge(y_ready, t + R - 1)
                for j, (s, m) in enumerate(HC):
                    last = mm(y_bank(t), hsT[0:m, g % 2, j, x:x + P], w2s[0:m, j, SH * D:(SH + 1) * D],
                              start=(j == 0), stop=(j == NHC - 1))
                last.then_inc(mm2_done, 1)

            def prefix():
                pe.wait_ge(sel_ready, 1)
                mm(ps_hi[:, 2, 0:(NT + 1) * E], before[:, :], sel[:, :, :], start=True, stop=False)
                for t in range(NT):
                    last = mm(ps_hi[:, 2, (t + 1) * E:(NT + 1) * E].rearrange("p (t e) -> p t e", e=E), ones_bf[:, :],
                              sel[:, t, :].unsqueeze(1).broadcast_to([P, NT - t, E]), start=False, stop=(t == NT - 1))
                last.then_inc(prefix_done, 1)

            def slot_tokens():
                pe.wait_ge(at_pos_ready, 1)
                pe.wait_ge(ids_ready, 1)
                for i in range(TOP * NT):
                    last = mm(ps_hi[:, 2, 0:4 * R], at_pos[:, i, :], ids[:, i, :], start=(i == 0),
                              stop=(i == TOP * NT - 1))
                last.then_inc(index_done, 1)

            for n in range(len(CHUNKS) - 1):
                embed(n)
            rows = [TT] * NA
            pe.wait_ge(consts_ready, 1)
            scores(0, TT)
            embed(len(CHUNKS) - 1)
            scores(1, TT)
            pe.wait_ge(hT_ready, C * len(CHUNKS))
            to_tokens(0, TT)
            for t in range(NA):
                if t >= 3:
                    h1_transpose(t - 3, TT)
                if t + 1 < NA:
                    if t >= 1:
                        scores(t + 1, rows[t + 1])
                    if t >= 3:
                        pe.wait_ge(v_ready, t + 1)
                        logits(t - 3)
                    to_tokens(t + 1, rows[t + 1])
                else:
                    pe.wait_ge(weights_loaded, 16 * 4 * NE)
                    shared_up(0, [0])
                if t >= 1:
                    z_transpose(t - 1, (t - 1) % 2, TT)
                attend(t, t % 2, rows[t])
            h1_transpose(NA - 3, TT)
            shared_up(0, [1])
            z_transpose(NA - 1, (NA - 1) % 2, TT)
            pe.wait_ge(v_ready, NA)
            logits(NA - 4)
            h1_transpose(NA - 2, TT)
            logits(NA - 3)
            shared_up(1)
            h1_transpose(NA - 1, TT)
            logits(NA - 2)
            logits(NA - 1)
            shared_up(2)
            shared_up(3)
            shared_down(0)
            prefix()
            shared_up(4)
            shared_down(1)
            shared_up(5)
            shared_down(2)
            slot_tokens()
            for i in range(6, UF):
                shared_up(i)
            shared_down(3)
            shared_down(4)
            pe.wait_ge(eid_ready, 1)
            x_transpose(0, 0)
            shared_down(5)
            x_transpose(1, 1)
            up(0, 0)
            up(1, 1)
            x_transpose(2, 0)
            hid_transpose(0, 0)
            for r in range(2, LOOP0):
                step(r, r % 2)
            with pe.Fori(LOOP0, LOOP1 - 1, 2) as r:
                step(r, 0)
                step(r + 1, 1)
            for r in range(LOOP1, R):
                step(r, r % 2)

            def begin_sum(t):
                pe.wait_ge(y_ready, shared_place(t) + 1)
                mm(sum_of(t), ident[:, :], acc[:, t, :], start=True, stop=False)

            def end_sum(t):
                pe.wait_ge(yg_loaded[t], 16)
                for k in range(TOP):
                    last = mm(sum_of(t), diag[:, t - DT, k, :], yg[:, t, k, :], start=False, stop=(k == TOP - 1))
                last.then_inc(sum_done, 1)

            shared_up(UF)
            hid_transpose(R - 1, (R - 1) % 2)
            down(R - 2, (R - 2) % 2)
            pe.wait_ge(diag_ready, TOP * (NT - DT))
            begin_sum(DT)
            down(R - 1, (R - 1) % 2)
            shared_up(UF + 1)
            pe.wait_ge(sgated_ready, UNITS - 1)
            begin_sum(DT + 1)
            begin_sum(DT + 2)
            for t in range(SF, NT):
                shared_down(t)
            pe.wait_ge(sgated_ready, UNITS)
            for t in range(DT + 3, NT):
                begin_sum(t)
            for t in range(DT, NT):
                end_sum(t)


_IN = ["patches_T", "tok_wT", "tok_b", "bq", "bk", "bv_row", "gate_wT", "gate_b", "w1", "b1", "w3", "b3",
       "w2", "b2", "sw1", "sw3", "sb13_T", "sw2", "sb2"]


def kernel(**inputs):
    import numpy as np
    import concourse.bacc as bacc
    from concourse.bass_utils import run_bass_kernel_spmd

    a = {n.replace("L0_", ""): np.asarray(x) for n, x in inputs.items()}
    B, C, H, W = a["x"].shape
    PS = 16
    h, w = H // PS, W // PS
    D = a["tok_W"].shape[0]
    laid = {
        "patches_T": a["x"].reshape(B, C, h, PS, w, PS).transpose(1, 3, 5, 0, 2, 4).reshape(C * PS * PS, B * h * w),
        "tok_wT": a["tok_W"].T,
        "tok_b": a["tok_b"].reshape(D // P, P).T,
        "bq": a["attn_bv_q"].reshape(D // P, P).T,
        "bk": a["attn_bv_k"].reshape(D // P, P).T,
        "bv_row": a["attn_bv_v"].reshape(D),
        "gate_wT": a["ffn_gate_w"].T,
        "sb13_T": np.stack([np.pad(a["ffn_" + n], (0, -len(a["ffn_" + n]) % P)).reshape(-1, P).T
                            for n in ("sb1", "sb3")], axis=1),
        **{n: a["ffn_" + n] for n in _IN[7:] if n != "sb13_T"},
    }
    nc = bacc.Bacc("TRN2", target_bir_lowering=False, num_devices=1)
    arrays, args = {}, []
    for n in _IN:
        x = np.ascontiguousarray(laid[n])
        arrays[f"in_{n}"] = x
        args.append(nc.dram_tensor(f"in_{n}", x.shape, mybir.dt.from_np(x.dtype), kind="ExternalInput").ap())
    out = nc.dram_tensor("out", (B * h * w, D), F32, kind="ExternalOutput").ap()
    vit_layer(nc, *args, out)
    r = run_bass_kernel_spmd(nc, [arrays], core_ids=[0])
    return r.results[0]["out"].reshape(B, h * w, D)
```
